# Optimizing a Trainium2 kernel written in Bass

```python
import numpy as np
import jax
import jax.numpy as jnp

def _softmax(x, axis=-1):
    return jax.nn.softmax(x, axis=axis)

def _gelu(x):
    return jax.nn.gelu(x, approximate=True)

def _silu(x):
    return jax.nn.silu(x)

def _sigmoid(x):
    return jax.nn.sigmoid(x)

def _layernorm(x, axis=-1, eps=1e-05):
    m = jnp.mean(x, axis=axis, keepdims=True)
    v = jnp.var(x, axis=axis, keepdims=True)
    return (x - m) / jnp.sqrt(v + eps)

def _scatter_add(tgt, idx, src, axis=0):
    return tgt.at[idx].add(src)

def _segment_sum(src, seg, n):
    return jax.ops.segment_sum(src, seg, n)
kernel_name = 'mk_decoder_postln_d1_seqx_r4_c4b664'

def setup_inputs(seed: int=0):
    np.random.seed(seed)
    _w = jnp.asarray

    def _rec_inputs():
        import jax
        import jax.numpy as jnp
        _rk = jax.random.key(seed)
        x = 0.5 + 0.2887 * jax.random.normal(jax.random.fold_in(_rk, 1), (4, 512, 512), jnp.float32)
        _lenS = 512 - jax.random.randint(jax.random.fold_in(_rk, 7), (4,), 0, max(1, 512 // 4) + 1, jnp.int32)
        _lenS2 = 512 - jax.random.randint(jax.random.fold_in(_rk, 8), (4,), 0, max(1, 512 // 4) + 1, jnp.int32)
        _ctx_512P = jax.random.normal(jax.random.fold_in(_rk, 11), (4, 16, 128), jnp.float32)
        _ctx_512c = jax.random.dirichlet(jax.random.fold_in(_rk, 511), 0.3 * jnp.ones((16,), jnp.float32), (4, 512))
        _ctx_512t = jnp.einsum('bsk,bkd->bsd', _ctx_512c, _ctx_512P)
        _ctx_512t = _ctx_512t * jax.lax.rsqrt(jnp.mean(jnp.square(_ctx_512t)) + 1e-12) * 0.953939
        ctx_512 = -0.000392918 + 0.999932 * (_ctx_512t + 0.3 * jax.random.normal(jax.random.fold_in(_rk, 611), (4, 512, 128), jnp.float32))
        return (x, ctx_512)
    x, ctx_512 = _rec_inputs()

    def _L0_attn_setup():
        import jax, jax.numpy as jnp
        import numpy as np
        B, T, H = (4, 512, 512)

        def _wkv(time_decay, time_first, k, v):
            td = -jnp.exp(time_decay.astype(jnp.float32))
            tf = time_first.astype(jnp.float32)
            kT = jnp.swapaxes(k, 0, 1).astype(jnp.float32)
            vT = jnp.swapaxes(v, 0, 1).astype(jnp.float32)
            bd = (k.shape[0], k.shape[2])
            init = (jnp.zeros(bd, jnp.float32), jnp.zeros(bd, jnp.float32), jnp.full(bd, -1e+38, jnp.float32))

            def step(carry, kv_t):
                num, den, mx = carry
                kt, vt = kv_t
                mfo = jnp.maximum(mx, kt + tf)
                e1 = jnp.exp(mx - mfo)
                e2 = jnp.exp(kt + tf - mfo)
                out = (e1 * num + e2 * vt) / (e1 * den + e2)
                mfs = jnp.maximum(mx + td, kt)
                e1s = jnp.exp(mx + td - mfs)
                e2s = jnp.exp(kt - mfs)
                return ((e1s * num + e2s * vt, e1s * den + e2s, mfs), out)
            _, outT = jax.lax.scan(step, init, (kT, vT))
            return jnp.swapaxes(outT, 0, 1).astype(k.dtype)
        key = jax.random.key(seed)
        ks = jax.random.split(key, 10)
        s = 0.02
        return {'hidden': jax.random.normal(ks[0], (B, T, H), jnp.float32), 'time_decay': jax.random.normal(ks[1], (H,), jnp.float32), 'time_first': jax.random.normal(ks[2], (H,), jnp.float32), 'time_mix_key': jax.random.uniform(ks[3], (1, 1, H), jnp.float32), 'time_mix_value': jax.random.uniform(ks[4], (1, 1, H), jnp.float32), 'time_mix_receptance': jax.random.uniform(ks[5], (1, 1, H), jnp.float32), 'Wk': jax.random.normal(ks[6], (H, H), jnp.float32) * s, 'Wv': jax.random.normal(ks[7], (H, H), jnp.float32) * s, 'Wr': jax.random.normal(ks[8], (H, H), jnp.float32) * s, 'Wo': jax.random.normal(ks[9], (H, H), jnp.float32) * s}
    _L0_attn_all = _L0_attn_setup()
    _L0_attn_in = {k: v for k, v in _L0_attn_all.items() if k in ('time_decay', 'time_first', 'time_mix_key', 'time_mix_value', 'time_mix_receptance', 'Wk', 'Wv', 'Wr', 'Wo')}
    del _L0_attn_all

    def _L0_xattn_setup():
        import jax, jax.numpy as jnp
        import numpy as np
        B, N, D = (16, 512, 128)
        H = 4
        TOP_K_RATIO = 0.3
        key = jax.random.key(seed)
        k1, k2, k3, k4 = jax.random.split(key, 4)
        h = jax.random.normal(k1, (B, N, D), dtype=jnp.float32)
        adj_raw = jax.random.uniform(k2, (B, N, N), dtype=jnp.float32)
        lim = 1.0 / np.sqrt(D)
        Wq = jax.random.uniform(k3, (D, D), minval=-lim, maxval=lim, dtype=jnp.float32)
        Wk = jax.random.uniform(k4, (D, D), minval=-lim, maxval=lim, dtype=jnp.float32)
        gamma_raw = jnp.float32(-0.85)
        return {'h': h, 'adj_raw': adj_raw, 'Wq': Wq, 'Wk': Wk, 'gamma_raw': gamma_raw}
    _L0_xattn_all = _L0_xattn_setup()
    _L0_xattn_in = {k: v for k, v in _L0_xattn_all.items() if k in ('Wq', 'Wk', 'gamma_raw')}
    del _L0_xattn_all

    def _L0_ffn_setup():
        import jax, jax.numpy as jnp
        import numpy as np
        import math
        B, S, D = (2, 512, 512)
        H, HD = (16, 128)
        E, I = (4, 512)
        TOP_K = 2
        ROPE_THETA = 10000.0

        def _layernorm(x, w, b):
            mu = jnp.mean(x, axis=-1, keepdims=True)
            var = jnp.mean(jnp.square(x - mu), axis=-1, keepdims=True)
            return (x - mu) * jax.lax.rsqrt(var + 1e-05) * w + b

        def _rotate_half(x):
            x1, x2 = jnp.split(x, 2, axis=-1)
            return jnp.concatenate((-x2, x1), axis=-1)

        def _attention(h, wq, bq, wk, bk, wv, bv, wo, bo):
            b, s, _ = h.shape
            q = (h @ wq + bq).reshape(b, s, H, HD).transpose(0, 2, 1, 3)
            k = (h @ wk + bk).reshape(b, s, H, HD).transpose(0, 2, 1, 3)
            v = (h @ wv + bv).reshape(b, s, H, HD).transpose(0, 2, 1, 3)
            inv_freq = 1.0 / ROPE_THETA ** (jnp.arange(0, HD, 2, dtype=jnp.float32) / HD)
            freqs = jnp.arange(s, dtype=jnp.float32)[:, None] * inv_freq[None, :]
            emb = jnp.concatenate((freqs, freqs), axis=-1)
            cos = jnp.cos(emb)[None, None]
            sin = jnp.sin(emb)[None, None]
            q = q * cos + _rotate_half(q) * sin
            k = k * cos + _rotate_half(k) * sin
            scores = jnp.einsum('bhqd,bhkd->bhqk', q, k) / math.sqrt(HD)
            causal = jnp.tril(jnp.ones((s, s), bool))
            scores = jnp.where(causal[None, None], scores, jnp.finfo(jnp.float32).min)
            probs = jax.nn.softmax(scores.astype(jnp.float32), axis=-1).astype(q.dtype)
            out = jnp.einsum('bhqk,bhkd->bhqd', probs, v)
            out = out.transpose(0, 2, 1, 3).reshape(b, s, H * HD)
            return out @ wo + bo

        def _moe(h, w_gate, we1, be1, we2, be2):
            b, s, d = h.shape
            x = h.reshape(-1, d)
            t = x.shape[0]
            raw = jax.nn.softmax(x @ w_gate, axis=-1)
            top_vals, top_idx = jax.lax.top_k(raw, TOP_K)
            w = jax.nn.softmax(top_vals, axis=-1)
            comb = jnp.zeros((t, E), x.dtype).at[jnp.arange(t)[:, None], top_idx].add(w)
            hmid = jax.nn.gelu(jnp.einsum('td,edi->tei', x, we1) + be1[None], approximate=False)
            eout = jnp.einsum('tei,eid->ted', hmid, we2) + be2[None]
            out = jnp.einsum('te,ted->td', comb, eout)
            return out.reshape(b, s, d)
        key = jax.random.key(seed)
        ks = jax.random.split(key, 20)
        s = 0.02
        p = {'hidden_states': jax.random.normal(ks[0], (B, S, D), jnp.float32), 'wq': jax.random.normal(ks[1], (D, H * HD), jnp.float32) * s, 'bq': jnp.zeros((H * HD,), jnp.float32), 'wk': jax.random.normal(ks[2], (D, H * HD), jnp.float32) * s, 'bk': jnp.zeros((H * HD,), jnp.float32), 'wv': jax.random.normal(ks[3], (D, H * HD), jnp.float32) * s, 'bv': jnp.zeros((H * HD,), jnp.float32), 'wo': jax.random.normal(ks[4], (H * HD, D), jnp.float32) * s, 'bo': jnp.zeros((D,), jnp.float32), 'ln1_w': jnp.ones((D,), jnp.float32), 'ln1_b': jnp.zeros((D,), jnp.float32), 'ln2_w': jnp.ones((D,), jnp.float32), 'ln2_b': jnp.zeros((D,), jnp.float32), 'w_gate': jax.random.normal(ks[5], (D, E), jnp.float32) * s, 'we1': jax.random.normal(ks[6], (E, D, I), jnp.float32) * s, 'be1': jnp.zeros((E, I), jnp.float32), 'we2': jax.random.normal(ks[7], (E, I, D), jnp.float32) * s, 'be2': jnp.zeros((E, D), jnp.float32)}
        return p
    _L0_ffn_all = _L0_ffn_setup()
    _L0_ffn_in = {k: v for k, v in _L0_ffn_all.items() if k in ('wq', 'bq', 'wk', 'bk', 'wv', 'bv', 'wo', 'bo', 'ln1_w', 'ln1_b', 'ln2_w', 'ln2_b', 'w_gate', 'we1', 'be1', 'we2', 'be2')}
    del _L0_ffn_all
    return {'x': x, 'ctx_512': ctx_512, 'L0_attn_time_decay': _L0_attn_in['time_decay'], 'L0_attn_time_first': _L0_attn_in['time_first'], 'L0_attn_time_mix_key': _L0_attn_in['time_mix_key'], 'L0_attn_time_mix_value': _L0_attn_in['time_mix_value'], 'L0_attn_time_mix_receptance': _L0_attn_in['time_mix_receptance'], 'L0_attn_Wk': _L0_attn_in['Wk'], 'L0_attn_Wv': _L0_attn_in['Wv'], 'L0_attn_Wr': _L0_attn_in['Wr'], 'L0_attn_Wo': _L0_attn_in['Wo'], 'L0_xattn_Wq': _L0_xattn_in['Wq'], 'L0_xattn_Wk': _L0_xattn_in['Wk'], 'L0_xattn_gamma_raw': _L0_xattn_in['gamma_raw'], 'L0_ffn_wq': _L0_ffn_in['wq'], 'L0_ffn_bq': _L0_ffn_in['bq'], 'L0_ffn_wk': _L0_ffn_in['wk'], 'L0_ffn_bk': _L0_ffn_in['bk'], 'L0_ffn_wv': _L0_ffn_in['wv'], 'L0_ffn_bv': _L0_ffn_in['bv'], 'L0_ffn_wo': _L0_ffn_in['wo'], 'L0_ffn_bo': _L0_ffn_in['bo'], 'L0_ffn_ln1_w': _L0_ffn_in['ln1_w'], 'L0_ffn_ln1_b': _L0_ffn_in['ln1_b'], 'L0_ffn_ln2_w': _L0_ffn_in['ln2_w'], 'L0_ffn_ln2_b': _L0_ffn_in['ln2_b'], 'L0_ffn_w_gate': _L0_ffn_in['w_gate'], 'L0_ffn_we1': _L0_ffn_in['we1'], 'L0_ffn_be1': _L0_ffn_in['be1'], 'L0_ffn_we2': _L0_ffn_in['we2'], 'L0_ffn_be2': _L0_ffn_in['be2']}

def reference(x, ctx_512, L0_attn_time_decay, L0_attn_time_first, L0_attn_time_mix_key, L0_attn_time_mix_value, L0_attn_time_mix_receptance, L0_attn_Wk, L0_attn_Wv, L0_attn_Wr, L0_attn_Wo, L0_xattn_Wq, L0_xattn_Wk, L0_xattn_gamma_raw, L0_ffn_wq, L0_ffn_bq, L0_ffn_wk, L0_ffn_bk, L0_ffn_wv, L0_ffn_bv, L0_ffn_wo, L0_ffn_bo, L0_ffn_ln1_w, L0_ffn_ln1_b, L0_ffn_ln2_w, L0_ffn_ln2_b, L0_ffn_w_gate, L0_ffn_we1, L0_ffn_be1, L0_ffn_we2, L0_ffn_be2):
    import jax
    import jax.numpy as jnp

    def _L0_attn_ref(hidden, time_decay, time_first, time_mix_key, time_mix_value, time_mix_receptance, Wk, Wv, Wr, Wo):
        import jax, jax.numpy as jnp
        import numpy as np
        B, T, H = (4, 512, 512)

        def _wkv(time_decay, time_first, k, v):
            td = -jnp.exp(time_decay.astype(jnp.float32))
            tf = time_first.astype(jnp.float32)
            kT = jnp.swapaxes(k, 0, 1).astype(jnp.float32)
            vT = jnp.swapaxes(v, 0, 1).astype(jnp.float32)
            bd = (k.shape[0], k.shape[2])
            init = (jnp.zeros(bd, jnp.float32), jnp.zeros(bd, jnp.float32), jnp.full(bd, -1e+38, jnp.float32))

            def step(carry, kv_t):
                num, den, mx = carry
                kt, vt = kv_t
                mfo = jnp.maximum(mx, kt + tf)
                e1 = jnp.exp(mx - mfo)
                e2 = jnp.exp(kt + tf - mfo)
                out = (e1 * num + e2 * vt) / (e1 * den + e2)
                mfs = jnp.maximum(mx + td, kt)
                e1s = jnp.exp(mx + td - mfs)
                e2s = jnp.exp(kt - mfs)
                return ((e1s * num + e2s * vt, e1s * den + e2s, mfs), out)
            _, outT = jax.lax.scan(step, init, (kT, vT))
            return jnp.swapaxes(outT, 0, 1).astype(k.dtype)
        shifted = jnp.pad(hidden, ((0, 0), (1, 0), (0, 0)))[:, :-1]
        key = hidden * time_mix_key + shifted * (1.0 - time_mix_key)
        value = hidden * time_mix_value + shifted * (1.0 - time_mix_value)
        rec = hidden * time_mix_receptance + shifted * (1.0 - time_mix_receptance)
        k = key @ Wk
        v = value @ Wv
        r = jax.nn.sigmoid(rec @ Wr)
        rwkv = _wkv(time_decay, time_first, k, v)
        return r * rwkv @ Wo

    def _L0_xattn_ref(h, adj_raw, Wq, Wk, gamma_raw):
        import jax, jax.numpy as jnp
        import numpy as np
        B, N, D = (16, 512, 128)
        H = 4
        TOP_K_RATIO = 0.3
        b, n, dm = h.shape
        d = dm // H
        Q = (h @ Wq.T).reshape(b, n, H, d).transpose(0, 2, 1, 3)
        K = (h @ Wk.T).reshape(b, n, H, d).transpose(0, 2, 1, 3)
        sim = jnp.einsum('bhnd,bhmd->bnm', Q, K) / (jnp.sqrt(jnp.float32(d)) * H)
        k = max(1, int(n * TOP_K_RATIO))
        topk_vals = jax.lax.top_k(sim, k)[0]
        threshold = topk_vals[:, :, -1:]
        sparse_mask = (sim >= threshold).astype(sim.dtype)
        A_learned = jax.nn.sigmoid(sim) * sparse_mask
        A_learned = (A_learned + jnp.swapaxes(A_learned, -1, -2)) * 0.5
        gamma = jax.nn.sigmoid(gamma_raw)
        return (1.0 - gamma) * adj_raw + gamma * A_learned

    def _L0_ffn_ref(hidden_states, wq, bq, wk, bk, wv, bv, wo, bo, ln1_w, ln1_b, ln2_w, ln2_b, w_gate, we1, be1, we2, be2):
        import jax, jax.numpy as jnp
        import numpy as np
        import math
        B, S, D = (2, 512, 512)
        H, HD = (16, 128)
        E, I = (4, 512)
        TOP_K = 2
        ROPE_THETA = 10000.0

        def _layernorm(x, w, b):
            mu = jnp.mean(x, axis=-1, keepdims=True)
            var = jnp.mean(jnp.square(x - mu), axis=-1, keepdims=True)
            return (x - mu) * jax.lax.rsqrt(var + 1e-05) * w + b

        def _rotate_half(x):
            x1, x2 = jnp.split(x, 2, axis=-1)
            return jnp.concatenate((-x2, x1), axis=-1)

        def _attention(h, wq, bq, wk, bk, wv, bv, wo, bo):
            b, s, _ = h.shape
            q = (h @ wq + bq).reshape(b, s, H, HD).transpose(0, 2, 1, 3)
            k = (h @ wk + bk).reshape(b, s, H, HD).transpose(0, 2, 1, 3)
            v = (h @ wv + bv).reshape(b, s, H, HD).transpose(0, 2, 1, 3)
            inv_freq = 1.0 / ROPE_THETA ** (jnp.arange(0, HD, 2, dtype=jnp.float32) / HD)
            freqs = jnp.arange(s, dtype=jnp.float32)[:, None] * inv_freq[None, :]
            emb = jnp.concatenate((freqs, freqs), axis=-1)
            cos = jnp.cos(emb)[None, None]
            sin = jnp.sin(emb)[None, None]
            q = q * cos + _rotate_half(q) * sin
            k = k * cos + _rotate_half(k) * sin
            scores = jnp.einsum('bhqd,bhkd->bhqk', q, k) / math.sqrt(HD)
            causal = jnp.tril(jnp.ones((s, s), bool))
            scores = jnp.where(causal[None, None], scores, jnp.finfo(jnp.float32).min)
            probs = jax.nn.softmax(scores.astype(jnp.float32), axis=-1).astype(q.dtype)
            out = jnp.einsum('bhqk,bhkd->bhqd', probs, v)
            out = out.transpose(0, 2, 1, 3).reshape(b, s, H * HD)
            return out @ wo + bo

        def _moe(h, w_gate, we1, be1, we2, be2):
            b, s, d = h.shape
            x = h.reshape(-1, d)
            t = x.shape[0]
            raw = jax.nn.softmax(x @ w_gate, axis=-1)
            top_vals, top_idx = jax.lax.top_k(raw, TOP_K)
            w = jax.nn.softmax(top_vals, axis=-1)
            comb = jnp.zeros((t, E), x.dtype).at[jnp.arange(t)[:, None], top_idx].add(w)
            hmid = jax.nn.gelu(jnp.einsum('td,edi->tei', x, we1) + be1[None], approximate=False)
            eout = jnp.einsum('tei,eid->ted', hmid, we2) + be2[None]
            out = jnp.einsum('te,ted->td', comb, eout)
            return out.reshape(b, s, d)
        a = _attention(_layernorm(hidden_states, ln1_w, ln1_b), wq, bq, wk, bk, wv, bv, wo, bo)
        h = hidden_states + a
        m = _moe(_layernorm(h, ln2_w, ln2_b), w_gate, we1, be1, we2, be2)
        return h + m
    x = _layernorm(x + _L0_attn_ref(x, L0_attn_time_decay, L0_attn_time_first, L0_attn_time_mix_key, L0_attn_time_mix_value, L0_attn_time_mix_receptance, L0_attn_Wk, L0_attn_Wv, L0_attn_Wr, L0_attn_Wo), axis=-1)
    x = _layernorm(x + _L0_xattn_ref(ctx_512, x, L0_xattn_Wq, L0_xattn_Wk, L0_xattn_gamma_raw), axis=-1)
    x = _layernorm(x + _L0_ffn_ref(x, L0_ffn_wq, L0_ffn_bq, L0_ffn_wk, L0_ffn_bk, L0_ffn_wv, L0_ffn_bv, L0_ffn_wo, L0_ffn_bo, L0_ffn_ln1_w, L0_ffn_ln1_b, L0_ffn_ln2_w, L0_ffn_ln2_b, L0_ffn_w_gate, L0_ffn_we1, L0_ffn_be1, L0_ffn_we2, L0_ffn_be2), axis=-1)
    return x

_drawn_inputs = setup_inputs


def setup_inputs(seed=0):
    import zlib

    import numpy as np

    out = dict(_drawn_inputs(seed))
    spreads = {'L0_ffn_bq': (0.0, 0.8),
     'L0_ffn_bk': (0.0, 0.8),
     'L0_ffn_bv': (0.0, 0.1),
     'L0_ffn_bo': (0.0, 0.1),
     'L0_ffn_ln1_w': (1.0, 0.6),
     'L0_ffn_ln1_b': (0.0, 0.325),
     'L0_ffn_ln2_w': (1.0, 0.6),
     'L0_ffn_ln2_b': (0.0, 0.529),
     'L0_ffn_be1': (0.0, 0.8),
     'L0_ffn_be2': (0.0, 0.1)}
    factors = {'L0_attn_time_decay': 3.082,
     'L0_attn_time_first': 3.106,
     'L0_attn_time_mix_key': 8.0,
     'L0_attn_time_mix_value': 2.976,
     'L0_attn_time_mix_receptance': 8.0,
     'L0_attn_Wk': 8.0,
     'L0_ffn_wq': 8.0,
     'L0_ffn_wk': 8.0}
    for name, (base, spread) in spreads.items():
        noise = np.random.default_rng([zlib.crc32(name.encode()), seed]).standard_normal(out[name].shape)
        drawn = base * np.exp(spread * noise) if base else spread * noise
        out[name] = jnp.asarray(drawn.astype(out[name].dtype))
    for name, factor in factors.items():
        out[name] = (out[name] * factor).astype(out[name].dtype)
    return out
```

```python
from contextlib import ExitStack

import numpy as np

import concourse.bass as bass
from concourse import mybir

F32 = mybir.dt.float32
ALU = mybir.AluOpType
ACT = mybir.ActivationFunctionType
AX = mybir.AxisListType

P = 128
B, T, D = 4, 512, 512
C = D // P
TC = T // P
HEADS = 16
GH = 4
NG = HEADS // GH
E = 4
DM = 128
XHEADS = 4
TOPK = int(T * 0.3)
ROUNDS = -(-TOPK // 8)
RPG = ROUNDS // NG
KTH = (TOPK - 1) % 8
assert ROUNDS == RPG * NG
EPS = 1e-5
SIM_SCALE = float(1.0 / (np.sqrt(np.float32(DM // XHEADS)) * XHEADS))
NEG = -1e30
MX0 = -1e38

COL = {}
_n = 0
for _name, _w in [("mix", 12), ("decay", 4), ("first", 4), ("bq", 16), ("bk", 16), ("bv", 16),
                  ("ln1w", 4), ("ln1b", 4), ("ln2w", 4), ("ln2b", 4), ("be1", 16), ("gamma", 1)]:
    COL[_name] = _n
    _n += _w
NCOL = _n


def block_a(nc, dram, x1_d, sim_d):
    with ExitStack() as ctx:
        def sb(name, shape):
            return ctx.enter_context(nc.sbuf_tensor(name, shape, F32))

        def sem(name):
            return ctx.enter_context(nc.semaphore(name))

        W = sb("W", [P, 4, C, D])
        vec = sb("vecA", [P, NCOL])
        omm = sb("omm", [P, 12])
        td = sb("td", [P, C])
        wqk = sb("wqk", [P, 2, DM])
        xT = sb("xT", [P, C, T + 1])
        xr = sb("xr", [P, TC, D])
        cT = sb("cT", [P, T])
        tmp = sb("tmp", [P, 2, 3, T])
        mk = sb("mk", [P, 3, C, T])
        qk = sb("qkA", [P, 2, T])
        sim = sb("simA", [P, TC, T])
        Mx = sb("Mx", [P, T + 1])
        dg = sb("dg", [P, 2, 2, T])
        rr = sb("rr", [P, 2, 2, T])
        ee = sb("ee", [P, 2, 4, T])
        Dn = sb("Dn", [P, 2, T + 1])
        Nm = sb("Nm", [P, 2, T + 1])
        vs = sb("vs", [P, 2, T])
        th = sb("th", [P, 2, T])
        ev = sb("ev", [P, 2, T])
        p2 = sb("p2", [P, 2, T])
        q1 = sb("q1", [P, 2, T])
        p1 = sb("p1", [P, 2, T])
        den = sb("den", [P, T])
        num = sb("num", [P, T])
        rec = sb("rec", [P, T])
        num2 = sb("num2", [P, T])
        rw = sb("rw", [P, C, T])
        z = sb("z", [P, TC, D])
        st = sb("stA", [P, TC, 6])
        mv = sb("mvA", [P, TC, 2])
        var = sb("varA", [P, TC])
        mhalf = sb("mhalfA", [P, TC])
        rstd = sb("rstdA", [P, TC])
        x1 = sb("x1A", [P, TC, D])
        ps = ctx.enter_context(nc.psum_tensor("psA", [P, 8, 512], F32))
        E1, E2S, E2, E1S = 0, 1, 2, 3
        Y = 6

        s_const = sem("a_const")
        s_xT = sem("a_xT")
        s_xr = sem("a_xr")
        s_cT = sem("a_cT")
        s_pre = sem("a_pre")
        s_half = sem("a_half")
        s_sh = sem("a_sh")
        s_mix = sem("a_mix")
        s_proj = sem("a_proj")
        s_dg = sem("a_dg")
        s_vt = sem("a_vt")
        s_e = sem("a_e")
        s_ev = sem("a_ev")
        s_scan = sem("a_scan")
        s_pq = sem("a_pq")
        s_rw = sem("a_rw")
        s_sps = sem("a_sps")
        s_sev = sem("a_sev")
        s_y = sem("a_y")
        s_z = sem("a_z")
        s_var = sem("a_var")
        s_rstd = sem("a_rstd")
        s_x1 = sem("a_x1")
        s_x1o = sem("a_x1o")
        s_simo = sem("a_simo")

        block = ctx.enter_context(nc.Block())

        @block.sync
        def _(sp):
            sp.dma_start(xT[:, :, :], dram["xT"][0]).then_inc(s_xT, 16)
            sp.dma_start(vec[:, :], dram["vec"]).then_inc(s_const, 16)
            sp.dma_start(wqk[:, :, :], dram["wqkT"]).then_inc(s_const, 16)
            for i in range(4):
                sp.dma_start(W[:, i, :, :], dram["W"][i]).then_inc(s_const, 16)
            sp.sem_inc(s_x1o, 16)
            sp.sem_inc(s_simo, 16)
            with sp.Fori(0, B) as b:
                sp.wait_ge(s_mix, 12 * b + 18)
                sp.dma_start(xT[:, :, :], dram["xT"][(b + 1) % B]).then_inc(s_xT, 16)
                sp.wait_ge(s_sev, 6 * b + 6)
                sp.dma_start(sim_d[b], sim[:, :, :]).then_inc(s_simo, 16)
                sp.wait_ge(s_x1, b + 1)
                sp.dma_start(x1_d[b], x1[:, :, :]).then_inc(s_x1o, 16)
            sp.wait_ge(s_simo, 16 * B + 16)
            sp.wait_ge(s_x1o, 16 * B + 16)
            sp.wait_ge(s_xT, 16 * B + 16)

        @block.gpsimd
        def _(pool):
            nc.gpsimd.memset(mhalf[:, :], -0.5).then_inc(s_half, 1)
            pool.wait_ge(s_half, 1)
            pool.dma_start(cT[:, :], dram["cT"][0]).then_inc(s_cT, 16)
            pool.dma_start(xr[:, :, :], dram["x"][0]).then_inc(s_xr, 16)

            def ev_products(b, c):
                i = c % 2
                pool.wait_ge(s_vt, 4 * b + c + 3)
                pool.wait_ge(s_e, 4 * b + c + 1)
                nc.gpsimd.tensor_tensor(ev[:, i, :], ee[:, i, E2S, :], vs[:, i, :], ALU.mult).then_inc(s_ev, 1)
                nc.gpsimd.tensor_tensor(p2[:, i, :], ee[:, i, E2, :], vs[:, i, :], ALU.mult).then_inc(s_ev, 1)

            def sum_products(b, c):
                i = c % 2
                pool.wait_ge(s_scan, 4 * b + c + 1)
                nc.gpsimd.tensor_tensor(q1[:, i, :], ee[:, i, E1, :], Dn[:, i, 0:T], ALU.mult).then_inc(s_pq, 1)
                nc.gpsimd.tensor_tensor(p1[:, i, :], ee[:, i, E1, :], Nm[:, i, 0:T], ALU.mult).then_inc(s_pq, 1)

            with pool.Fori(0, B) as b:
                for c in range(C + 1):
                    if c < C:
                        ev_products(b, c)
                    if c >= 1:
                        sum_products(b, c - 1)
                pool.wait_ge(s_sps, 6 * b + 6)
                pool.dma_start(cT[:, :], dram["cT"][(b + 1) % B]).then_inc(s_cT, 16)
                pool.wait_ge(s_var, b + 1)
                nc.gpsimd.tensor_tensor(rstd[:, :], var[:, :], mhalf[:, :], ALU.pow).then_inc(s_rstd, 1)
                pool.wait_ge(s_z, 4 * b + 8)
                pool.dma_start(xr[:, :, :], dram["x"][(b + 1) % B]).then_inc(s_xr, 16)
            pool.wait_ge(s_cT, 16 * B + 16)
            pool.wait_ge(s_xr, 16 * B + 16)

        @block.scalar
        def _(act):
            act.wait_ge(s_const, 96)
            nc.scalar.activation(td[:, :], vec[:, COL["decay"]:COL["decay"] + C], ACT.Exp).then_inc(s_pre, 1)
            act.wait_ge(s_pre, 5)
            act.sem_inc(s_vt, 2)

            def shift_parts(bm, c):
                act.wait_ge(s_mix, 12 * bm + 3 * c + 6)
                for m in range(3):
                    nc.scalar.mul(tmp[:, c % 2, m, :], xT[:, c, 0:T], omm[:, 4 * m + c:4 * m + c + 1]).then_inc(s_sh, 1)

            def chunk(b, c):
                i = c % 2
                act.wait_ge(s_rw, 4 * b + c + 3)
                act.wait_ge(s_proj, 12 * b + 3 * c + 2)
                nc.scalar.copy(vs[:, i, :], ps[:, 3 * i + 1, :])
                act.wait_ge(s_proj, 12 * b + 3 * c + 3)
                nc.scalar.activation(th[:, i, :], ps[:, 3 * i + 2, :], ACT.Tanh, scale=0.5).then_inc(s_vt, 1)
                act.drain()
                act.wait_ge(s_dg, 4 * b + c + 3)
                nc.scalar.activation(rr[:, 0, :, :], dg[:, i, :, :], ACT.Relu)
                nc.scalar.activation(rr[:, 1, :, :], dg[:, i, :, :], ACT.Relu, scale=-1.0)
                act.drain()
                nc.scalar.activation(ee[:, i, :, :].rearrange("p a t -> p (a t)"),
                                     rr[:, :, :, :].rearrange("p a c t -> p (a c t)"), ACT.Exp,
                                     scale=-1.0).then_inc(s_e, 1)

            act.wait_ge(s_xT, 16)
            for c in range(C):
                shift_parts(0, c)
            with act.Fori(0, B) as b:
                chunk(b, 0)
                chunk(b, 1)
                act.wait_ge(s_simo, 16 * b + 16)
                for j in range(2):
                    act.wait_ge(s_sps, 6 * b + j + 1)
                    nc.scalar.copy(qk[:, j, :], ps[:, Y + j, :]).then_inc(s_sev, 1)
                for t in range(TC):
                    act.wait_ge(s_sps, 6 * b + t + 3)
                    nc.scalar.mul(sim[:, t, :], ps[:, Y + t % 2, :], SIM_SCALE).then_inc(s_sev, 1)
                chunk(b, 2)
                chunk(b, 3)
                act.wait_ge(s_xT, 16 * b + 32)
                for c in range(C):
                    shift_parts(b + 1, c)

        @block.vector
        def _(dve):
            v = nc.vector
            v.memset(Mx[:, 0:1], MX0).then_inc(s_pre, 1)
            v.memset(Dn[:, :, 0:1], 0.0).then_inc(s_pre, 1)
            v.memset(Nm[:, :, 0:1], 0.0).then_inc(s_pre, 1)
            dve.wait_ge(s_const, 96)
            v.tensor_scalar(omm[:, :], vec[:, 0:12], -1.0, 1.0, ALU.mult, ALU.add).then_inc(s_pre, 1)
            dve.wait_ge(s_pre, 5)
            v.tensor_scalar(td[:, :], td[:, :], -1.0, None, ALU.mult)
            dve.sem_inc(s_mix, 6)
            dve.sem_inc(s_dg, 2)
            dve.sem_inc(s_rw, 4)
            dve.sem_inc(s_z, 4)

            def mixes(bm):
                for c in range(C):
                    for m in range(3):
                        dve.wait_ge(s_sh, 12 * bm + 3 * c + m + 1)
                        v.scalar_tensor_tensor(mk[:, m, c, :], xT[:, c, 1:T + 1],
                                               vec[:, COL["mix"] + 4 * m + c:COL["mix"] + 4 * m + c + 1],
                                               tmp[:, c % 2, m, :], ALU.mult, ALU.add).then_inc(s_mix, 1)

            def exponents(b, c):
                k = ps[:, 3 * (c % 2), :]
                v.drain()
                dve.wait_ge(s_proj, 12 * b + 3 * c + 1)
                v.tensor_tensor_scan(Mx[:, 1:T + 1], td[:, c:c + 1].to_broadcast([P, T]), k, MX0, ALU.add, ALU.max)
                v.drain()
                v.scalar_tensor_tensor(dg[:, c % 2, 0, :], k, vec[:, COL["first"] + c:COL["first"] + c + 1],
                                       Mx[:, 0:T], ALU.add, ALU.subtract)
                v.scalar_tensor_tensor(dg[:, c % 2, 1, :], Mx[:, 0:T], td[:, c:c + 1], k, ALU.add,
                                       ALU.subtract).then_inc(s_dg, 1)

            def sums(b, c):
                i = c % 2
                dve.wait_ge(s_e, 4 * b + c + 1)
                v.tensor_tensor_scan(Dn[:, i, 1:T + 1], ee[:, i, E1S, :], ee[:, i, E2S, :], 0.0, ALU.mult, ALU.add)
                dve.wait_ge(s_ev, 8 * b + 2 * c + 1)
                v.tensor_tensor_scan(Nm[:, i, 1:T + 1], ee[:, i, E1S, :], ev[:, i, :], 0.0, ALU.mult,
                                     ALU.add).then_inc(s_scan, 1)

            def outputs(b, c):
                i = c % 2
                v.drain()
                dve.wait_ge(s_pq, 8 * b + 2 * c + 2)
                v.tensor_tensor(den[:, :], q1[:, i, :], ee[:, i, E2, :], ALU.add)
                v.tensor_tensor(num[:, :], p1[:, i, :], p2[:, i, :], ALU.add)
                v.drain()
                v.reciprocal(rec[:, :], den[:, :])
                v.scalar_tensor_tensor(num2[:, :], th[:, i, :], 1.0, num[:, :], ALU.add, ALU.mult)
                v.drain()
                v.scalar_tensor_tensor(rw[:, c, :], num2[:, :], 0.5, rec[:, :], ALU.mult,
                                       ALU.mult).then_inc(s_rw, 1)

            dve.wait_ge(s_xT, 16)
            mixes(0)
            with dve.Fori(0, B) as b:
                exponents(b, 0)
                exponents(b, 1)
                sums(b, 0)
                for c in range(2, C):
                    exponents(b, c)
                    outputs(b, c - 2)
                    sums(b, c - 1)
                outputs(b, C - 2)
                sums(b, C - 1)
                outputs(b, C - 1)
                dve.wait_ge(s_proj, 12 * b + 12)
                mixes(b + 1)
                v.drain()
                dve.wait_ge(s_xr, 16 * b + 16)
                for t in range(TC):
                    dve.wait_ge(s_y, 4 * b + t + 1)
                    v.tensor_tensor(z[:, t, :], ps[:, Y + t % 2, :], xr[:, t, :], ALU.add).then_inc(s_z, 1)
                    v.drain()
                    v.bn_stats(st[:, t, :], z[:, t, :])
                v.drain()
                for t in range(TC):
                    v.bn_aggr(mv[:, t, :], st[:, t, :])
                v.drain()
                v.tensor_scalar(var[:, :], mv[:, :, 1], EPS, None, ALU.add).then_inc(s_var, 1)
                dve.wait_ge(s_x1o, 16 * b + 16)
                dve.wait_ge(s_rstd, b + 1)
                for t in range(TC):
                    ins = v.tensor_scalar(x1[:, t, :], z[:, t, :], mv[:, t, 0:1], rstd[:, t:t + 1],
                                          ALU.subtract, ALU.mult)
                ins.then_inc(s_x1, 1)

        @block.tensor
        def _(pe):
            mm = nc.tensor.matmul
            pe.wait_ge(s_const, 96)

            def project(b, c):
                pe.wait_ge(s_dg, 4 * b + c + 1)
                pe.wait_ge(s_vt, 4 * b + c + 1)
                if c == 0:
                    pe.wait_ge(s_mix, 12 * b + 18)
                for m in range(3):
                    for k in range(C):
                        ins = mm(ps[:, 3 * (c % 2) + m, :], W[:, m, k, c * P:(c + 1) * P], mk[:, m, k, :],
                                 start=(k == 0), stop=(k == C - 1))
                    ins.then_inc(s_proj, 1)

            with pe.Fori(0, B) as b:
                project(b, 0)
                project(b, 1)
                pe.wait_ge(s_cT, 16 * b + 16)
                for j in range(2):
                    pe.wait_ge(s_z, 4 * b + 3 + j)
                    mm(ps[:, Y + j, :], wqk[:, j, :], cT[:, :], start=True, stop=True).then_inc(s_sps, 1)
                pe.wait_ge(s_sev, 6 * b + 2)
                for t in range(TC):
                    if t >= 2:
                        pe.wait_ge(s_sev, 6 * b + t + 1)
                    mm(ps[:, Y + t % 2, :], qk[:, 0, t * P:(t + 1) * P], qk[:, 1, :], start=True,
                       stop=True).then_inc(s_sps, 1)
                project(b, 2)
                project(b, 3)
                pe.wait_ge(s_sev, 6 * b + 6)
                pe.wait_ge(s_rw, 4 * b + 8)
                for t in range(TC):
                    if t >= 2:
                        pe.wait_ge(s_z, 4 * b + t + 3)
                    for c in range(C):
                        ins = mm(ps[:, Y + t % 2, :], rw[:, c, t * P:(t + 1) * P], W[:, 3, c, :],
                                 start=(c == 0), stop=(c == C - 1))
                    ins.then_inc(s_y, 1)


def block_c(nc, dram, x1_d, sim_d, out):
    with ExitStack() as ctx:
        def sb(name, shape):
            return ctx.enter_context(nc.sbuf_tensor(name, shape, F32))

        def sem(name):
            return ctx.enter_context(nc.semaphore(name))

        vec = sb("vec", [P, NCOL])
        ident = sb("ident", [P, P])
        rope = sb("rope", [P, 4, T])
        causal = sb("causal", [P, P])
        before = sb("before", [P, TC, E, E])
        bo = sb("bo", [P, D])
        wg = sb("wg", [P, C, E])
        be2 = sb("be2", [E, D])
        gam = sb("gam", [P, 4])
        mhalf = sb("mhalf", [P, TC])
        wa = sb("wa", [P, 4, C, GH * P])
        we = sb("we", [P, 2, C, D])
        tk = sb("tk", [P, TC, T])
        m8 = sb("m8", [P, TC, 8])
        thr = sb("thr", [P, TC])
        sx = sb("sx", [P, TC, T])
        tx = sb("tx", [P, TC, T])
        x1 = sb("x1", [P, TC, D])
        x2 = sb("x2", [P, TC, D])
        xn = sb("xn", [P, TC, D])
        xT = sb("xnT", [P, C, T])
        h = sb("h", [P, TC, D])
        st = sb("st", [P, TC, 6])
        mv = sb("mv", [P, TC, 2])
        var = sb("var", [P, TC])
        rstd = sb("rstd", [P, TC])
        sh = sb("sh", [P, 2, T])
        rc = sb("rc", [P, 2, T])
        rs_ = sb("rs_", [P, 2, T])
        qk = sb("qk", [P, 2, 2, T])
        Vg = sb("Vg", [P, TC, GH * P])
        Pr = sb("Pr", [P, TC, T])
        nmax = sb("nmax", [P, TC])
        rsum = sb("rsum", [P, TC])
        rinv = sb("rinv", [P, TC])
        PT = sb("PT", [P, TC, T])
        OT = sb("OT", [P, GH, T])
        hm = sb("hm", [P, 2, C, T])
        lg = sb("lg", [P, 6, TC, E])
        r1 = sb("r1", [P, 6, TC])
        cmp_ = sb("cmp", [P, 3, TC, E, E])
        combT = sb("combT", [E, T])
        ps = ctx.enter_context(nc.psum_tensor("ps", [P, 8, 512], F32))
        PJ, SA, SB, SC, PV = 0, 4, 5, 6, 7

        s_const = sem("c_const")
        s_pre = sem("c_pre")
        s_half = sem("c_half")
        s_tkin = sem("c_tkin")
        s_tkdone = sem("c_tkdone")
        s_xin = sem("c_xin")
        s_xth = sem("c_xth")
        s_xA = sem("c_xA")
        s_xAT = sem("c_xAT")
        s_xfree = sem("c_xfree")
        s_var = sem("c_var")
        s_rstd = sem("c_rstd")
        s_xn = sem("c_xn")
        s_nT = sem("c_nT")
        s_nTe = sem("c_nTe")
        s_w = [sem(f"c_w{i}") for i in range(4)]
        s_QK = sem("c_QK")
        s_V = sem("c_V")
        s_Ve = sem("c_Ve")
        s_sh = sem("c_sh")
        s_rs = sem("c_rs")
        s_rope = sem("c_rope")
        s_S = sem("c_S")
        s_nm = sem("c_nm")
        s_P = sem("c_P")
        s_Pn = sem("c_Pn")
        s_T = sem("c_T")
        s_PT = sem("c_PT")
        s_PV = sem("c_PV")
        s_OT = sem("c_OT")
        s_O = sem("c_O")
        s_Oe = sem("c_Oe")
        s_we = [sem(f"c_we{i}") for i in range(2)]
        s_lg = sem("c_lg")
        s_lge = sem("c_lge")
        s_lgx = sem("c_lgx")
        s_comb = sem("c_comb")
        s_cT = sem("c_cT")
        s_cTe = sem("c_cTe")
        s_h1 = sem("c_h1")
        s_gel = sem("c_gel")
        s_y = sem("c_y")
        s_ye = sem("c_ye")
        s_fin = sem("c_fin")
        s_out = sem("c_out")

        block = ctx.enter_context(nc.Block())

        @block.sync
        def _(sp):
            for dst, name in [(vec[:, :], "vec"), (ident[:, :], "ident"), (rope[:, :, :], "rope"),
                              (causal[:, :], "causal"), (before[:, :, :, :], "before"), (bo[:, :], "bo"),
                              (wg[:, :, :], "wg"), (be2[:, :], "be2")]:
                sp.dma_start(dst, dram[name]).then_inc(s_const, 16)
            sp.sem_inc(s_out, 16)
            with sp.Fori(0, B) as b:
                with sp.Fori(0, NG) as g:
                    G = b * NG + g
                    sp.wait_ge(s_QK, 8 * G + 8)
                    sp.dma_start(wa[:, 0, :, :], dram["wq"][g]).then_inc(s_w[0], 16)
                    sp.dma_start(wa[:, 1, :, :], dram["wk"][g]).then_inc(s_w[1], 16)
                    sp.wait_ge(s_O, 4 * G + 4)
                    sp.dma_start(wa[:, 3, :, :], dram["wo"][g]).then_inc(s_w[3], 16)
                for e in range(E):
                    sp.wait_ge(s_h1, 16 * b + 4 * e + 4)
                    sp.dma_start(we[:, 0, :, :], dram["we1"][e]).then_inc(s_we[0], 16)
                    sp.wait_ge(s_y, 20 * b + 4 * e + (8 if e else 4))
                    sp.dma_start(we[:, 1, :, :], dram["we2"][e]).then_inc(s_we[1], 16)
                sp.wait_ge(s_fin, b + 1)
                sp.dma_start(out[b], xn[:, :, :]).then_inc(s_out, 16)
            sp.wait_ge(s_out, 16 * B + 16)

        @block.gpsimd
        def _(pool):
            pool.dma_start(tk[:, :, :], sim_d[0]).then_inc(s_tkin, 16)
            nc.gpsimd.memset(mhalf[:, :], -0.5).then_inc(s_half, 1)
            pool.wait_ge(s_half, 1)
            pool.wait_ge(s_const, 128)

            def root(n):
                pool.wait_ge(s_var, n)
                nc.gpsimd.tensor_tensor(rstd[:, :], var[:, :], mhalf[:, :], ALU.pow).then_inc(s_rstd, 1)

            def sines(n, a):
                pool.wait_ge(s_sh, 2 * n + a + 1)
                nc.gpsimd.tensor_tensor(rs_[:, a, :], sh[:, a, :], rope[:, 2 * a + 1, :], ALU.mult).then_inc(s_rs, 1)

            with pool.Fori(0, B) as b:
                pool.wait_ge(s_xfree, b + 1)
                pool.dma_start(sx[:, :, :], sim_d[b]).then_inc(s_xin, 16)
                pool.dma_start(x1[:, :, :], x1_d[b]).then_inc(s_xin, 16)
                pool.wait_ge(s_tkdone, b + 1)
                pool.dma_start(tk[:, :, :], sim_d[(b + 1) % B]).then_inc(s_tkin, 16)
                root(4 * b + 1)
                root(4 * b + 2)
                with pool.Fori(0, NG) as g:
                    G = b * NG + g
                    pool.wait_ge(s_V, 4 * G + 4)
                    pool.dma_start(wa[:, 2, :, :], dram["wv"][g]).then_inc(s_w[2], 16)
                    for hh in range(GH):
                        sines(4 * G + hh, 0)
                        sines(4 * G + hh, 1)
                root(4 * b + 3)
                root(4 * b + 4)

        @block.scalar
        def _(act):
            A = nc.scalar.activation
            act.wait_ge(s_const, 128)
            A(gam[:, 2:3], vec[:, COL["gamma"]:COL["gamma"] + 1], ACT.Tanh, scale=0.5).then_inc(s_pre, 1)
            act.sem_inc(s_OT, 1)
            act.sem_inc(s_gel, 4)

            def col(name, i):
                return vec[:, COL[name] + i:COL[name] + i + 1]

            def swap_halves(n, head, a):
                bank = ps[:, PJ + {0: 0, 1: 2, 2: 0, 3: 2}[n % 4 if isinstance(n, int) else 0], :]
                return bank

            def swapped(G, hh, a):
                n = 4 * G + hh
                bank = PJ + 2 * (hh % 2) + a
                bias = vec[:, bass.ds(COL["bq"] + 16 * a + n_head(hh), 1)]
                act.wait_ge(s_QK, 8 * G + 8 + 2 * hh + a + 1)
                act.wait_ge(s_rope, 2 * n + 1 + a)
                A(sh[0:64, a, :], ps[64:128, bank, :], ACT.Identity, bias=bias[64:128, :])
                A(sh[64:128, a, :], ps[0:64, bank, :], ACT.Identity, bias=bias[0:64, :]).then_inc(s_sh, 1)

            def exps(n):
                for t in range(TC):
                    act.wait_ge(s_nm, 4 * n + max(t, 1) + 1)
                    A(Pr[:, t, 0:(t + 1) * P], s_tile(t), ACT.Exp, bias=nmax[:, t:t + 1],
                      accum_out=rsum[:, t:t + 1]).then_inc(s_P, 1)

            def s_tile(t):
                return [ps[:, SA, 0:P], ps[:, SA, P:3 * P], ps[:, SB, 0:3 * P], ps[:, SC, 0:4 * P]][t]

            def pt_out(n):
                act.wait_ge(s_T, 3 * n + 1)
                nc.scalar.copy(PT[:, 0, :], ps[:, SA, :]).then_inc(s_PT, 1)
                act.wait_ge(s_T, 3 * n + 2)
                nc.scalar.copy(PT[:, 1, P:T], ps[:, SB, 0:3 * P])
                nc.scalar.copy(PT[:, 3, 3 * P:T], ps[:, SB, 3 * P:T]).then_inc(s_PT, 1)
                act.wait_ge(s_T, 3 * n + 3)
                nc.scalar.copy(PT[:, 2, 2 * P:T], ps[:, SC, 0:2 * P]).then_inc(s_PT, 1)

            def ot_out(n, g, hh):
                act.wait_ge(s_PV, n + 1)
                A(OT[:, hh, :], ps[:, PV, :], ACT.Identity,
                  bias=vec[:, bass.ds(COL["bv"] + 4 * g + hh, 1)]).then_inc(s_OT, 1)

            def normed(b, which, lnw, lnb):
                for c in range(C):
                    act.wait_ge(s_nT, 8 * b + 4 * which + c + 1)
                    A(xT[:, c, :], ps[:, PJ + c, :], ACT.Identity, bias=col(lnb, c),
                      scale=col(lnw, c)).then_inc(s_nTe, 1)

            with act.Fori(0, B) as b:
                act.wait_ge(s_xin, 32 * b + 32)
                for t in range(TC):
                    A(tx[:, t, :], sx[:, t, :], ACT.Tanh, scale=0.5).then_inc(s_xth, 1)
                normed(b, 0, "ln1w", "ln1b")
                with act.Fori(0, NG) as g:
                    G = b * NG + g

                    def n_head(hh):
                        return 4 * g + hh
                    for hh in range(2):
                        swapped(G, hh, 0)
                        swapped(G, hh, 1)
                    for hh in range(GH):
                        n = 4 * G + hh
                        exps(n)
                        if hh == 0:
                            for t in range(TC):
                                act.wait_ge(s_V, 4 * G + 4 + t + 1)
                                nc.scalar.copy(Vg[:, t, :], ps[:, PJ + t, :]).then_inc(s_Ve, 1)
                        if 1 <= hh < 3:
                            swapped(G, hh + 1, 0)
                            swapped(G, hh + 1, 1)
                        pt_out(n)
                        ot_out(n, g, hh)
                normed(b, 1, "ln2w", "ln2b")
                for i in range(2):
                    act.wait_ge(s_lge, 2 * b + i + 1)
                    A(lg[:, 2 + 2 * i, :, :], lg[:, 1 + 2 * i, :, :], ACT.Exp).then_inc(s_lgx, 1)
                act.wait_ge(s_cT, b + 1)
                nc.scalar.copy(combT[:, :], ps[0:E, SB, :]).then_inc(s_cTe, 1)
                for e in range(E):
                    for i in range(C):
                        act.wait_ge(s_h1, 16 * b + 4 * e + i + 5)
                        A(hm[:, e % 2, i, :], ps[:, PJ + i, :], ACT.Gelu,
                          bias=col("be1", 4 * e + i)).then_inc(s_gel, 1)

        @block.vector
        def _(dve):
            v = nc.vector
            dve.wait_ge(s_const, 128)
            dve.wait_ge(s_pre, 1)
            v.tensor_scalar(gam[:, 0:1], gam[:, 2:3], 1.0, 0.125, ALU.add, ALU.mult)
            v.tensor_scalar(gam[:, 1:2], gam[:, 2:3], -0.5, 1.5, ALU.mult, ALU.add)
            dve.sem_inc(s_xfree, 1)
            dve.sem_inc(s_rope, 2)
            dve.sem_inc(s_Oe, 4)
            dve.sem_inc(s_ye, 4)

            def take_largest(tiles, rounds):
                for _ in range(rounds):
                    for t in tiles:
                        v.max(m8[:, t, :], tk[:, t, :])
                    v.drain()
                    for t in tiles:
                        v.match_replace(tk[:, t, :], m8[:, t, :], tk[:, t, :], NEG)
                    v.drain()

            def layer_norm(k, src, dst):
                v.drain()
                for t in range(TC):
                    v.bn_stats(st[:, t, :], src[:, t, :])
                v.drain()
                for t in range(TC):
                    v.bn_aggr(mv[:, t, :], st[:, t, :])
                v.drain()
                v.tensor_scalar(var[:, :], mv[:, :, 1], EPS, None, ALU.add).then_inc(s_var, 1)
                dve.wait_ge(s_rstd, k)
                for t in range(TC):
                    ins = v.tensor_scalar(dst[:, t, :], src[:, t, :], mv[:, t, 0:1], rstd[:, t:t + 1],
                                          ALU.subtract, ALU.mult)
                return ins

            def s_tile(t):
                return [ps[:, SA, 0:P], ps[:, SA, P:3 * P], ps[:, SB, 0:3 * P], ps[:, SC, 0:4 * P]][t]

            def rotate(G, g, hh, a):
                n = 4 * G + hh
                bank = PJ + 2 * (hh % 2) + a
                dve.wait_ge(s_sh, 2 * n + a + 1)
                v.scalar_tensor_tensor(rc[:, a, :], ps[:, bank, :], vec[:, bass.ds(COL["bq"] + 16 * a + 4 * g + hh, 1)],
                                       rope[:, 2 * a, :], ALU.add, ALU.mult)
                v.drain()
                dve.wait_ge(s_rs, 2 * n + a + 1)
                v.tensor_tensor(qk[:, hh % 2, a, :], rc[:, a, :], rs_[:, a, :], ALU.add).then_inc(s_rope, 1)

            def maxima(n):
                for t0 in (0, 2):
                    if t0 == 0:
                        dve.wait_ge(s_S, 4 * n + 2)
                    for t in (t0, t0 + 1):
                        if t0 == 2:
                            dve.wait_ge(s_S, 4 * n + t + 1)
                        diag = s_tile(t)[:, t * P:(t + 1) * P]
                        v.tensor_tensor(diag, diag, causal[:, :], ALU.add)
                    v.drain()
                    for t in (t0, t0 + 1):
                        v.tensor_reduce(nmax[:, t:t + 1], s_tile(t), AX.X, ALU.max, negate=True).then_inc(s_nm, 1)

            def normalise(n):
                for t0 in (0, 2):
                    dve.wait_ge(s_P, 4 * n + t0 + 2)
                    v.reciprocal(rinv[:, t0:t0 + 2], rsum[:, t0:t0 + 2])
                    v.drain()
                    for t in (t0, t0 + 1):
                        ins = v.tensor_scalar(Pr[:, t, 0:(t + 1) * P], Pr[:, t, 0:(t + 1) * P], rinv[:, t:t + 1],
                                              None, ALU.mult)
                ins.then_inc(s_Pn, 1)

            dve.wait_ge(s_tkin, 16)
            take_largest(range(TC), ROUNDS)
            with dve.Fori(0, B) as b:
                v.tensor_copy(thr[:, :], m8[:, :, KTH]).then_inc(s_tkdone, 1)
                v.drain()
                dve.wait_ge(s_xin, 32 * b + 32)
                for t in range(TC):
                    dve.wait_ge(s_xth, 4 * b + t + 1)
                    v.tensor_scalar(tx[:, t, :], tx[:, t, :], 1.0, None, ALU.add)
                v.drain()
                for t in range(TC):
                    v.scalar_tensor_tensor(sx[:, t, :], sx[:, t, :], thr[:, t:t + 1], tx[:, t, :], ALU.is_ge,
                                           ALU.mult).then_inc(s_xA, 1)
                v.drain()
                for t in range(TC):
                    dve.wait_ge(s_xAT, 4 * b + t + 1)
                    v.tensor_tensor(tx[:, t, :], ps[:, PJ + t, :], sx[:, t, :], ALU.add)
                v.drain()
                dve.wait_ge(s_out, 16 * b + 16)
                for t in range(TC):
                    v.tensor_scalar(tx[:, t, :], tx[:, t, :], gam[:, 0:1], None, ALU.mult)
                v.drain()
                for t in range(TC):
                    ins = v.scalar_tensor_tensor(x2[:, t, :], x1[:, t, :], gam[:, 1:2], tx[:, t, :], ALU.mult,
                                                 ALU.add)
                ins.then_inc(s_xfree, 1)
                layer_norm(4 * b + 1, x2, x2)
                layer_norm(4 * b + 2, x2, xn).then_inc(s_xn, 1)
                for t in range(TC):
                    v.tensor_tensor(h[:, t, :], x2[:, t, :], bo[:, :], ALU.add)
                with dve.Fori(0, NG) as g:
                    G = b * NG + g
                    dve.wait_ge(s_tkin, 16 * b + 32)
                    for hh in range(2):
                        rotate(G, g, hh, 0)
                        rotate(G, g, hh, 1)
                    for hh in range(GH):
                        n = 4 * G + hh
                        maxima(n)
                        take_largest([hh], 2)
                        normalise(n)
                        if 1 <= hh < 3:
                            rotate(G, g, hh + 1, 0)
                            rotate(G, g, hh + 1, 1)
                        take_largest([hh], RPG - 2)
                    for t in range(TC):
                        dve.wait_ge(s_O, 4 * G + t + 5)
                        v.tensor_tensor(h[:, t, :], ps[:, PJ + t, :], h[:, t, :], ALU.add).then_inc(s_Oe, 1)
                layer_norm(4 * b + 3, h, xn).then_inc(s_xn, 1)
                for t in range(TC):
                    v.tensor_tensor(x2[:, t, :], x2[:, t, :], h[:, t, :], ALU.add)

                def over(x):
                    return x.rearrange("p (t o) -> p t o", o=1).to_broadcast([P, TC, E])
                dve.wait_ge(s_lg, b + 1)
                v.tensor_copy(lg[:, 0, :, :], ps[:, SA, 0:TC * E].rearrange("p (t e) -> p t e", e=E))
                v.drain()
                v.tensor_reduce(r1[:, 0, :], lg[:, 0, :, :], AX.X, ALU.max)
                v.drain()
                v.tensor_tensor(lg[:, 1, :, :], lg[:, 0, :, :], over(r1[:, 0, :]), ALU.subtract).then_inc(s_lge, 1)
                dve.wait_ge(s_lgx, 2 * b + 1)
                v.tensor_reduce(r1[:, 1, :], lg[:, 2, :, :], AX.X, ALU.add)
                v.drain()
                v.reciprocal(r1[:, 2, :], r1[:, 1, :])
                v.drain()
                v.tensor_tensor(lg[:, 0, :, :], lg[:, 2, :, :], over(r1[:, 2, :]), ALU.mult)
                v.drain()
                v.tensor_reduce(r1[:, 3, :], lg[:, 0, :, :], AX.X, ALU.max)
                for j in range(E):
                    pj = lg[:, 0, :, j:j + 1].to_broadcast([P, TC, E])
                    v.tensor_tensor(cmp_[:, 0, :, :, j], pj, lg[:, 0, :, :], ALU.is_gt)
                    v.tensor_tensor(cmp_[:, 1, :, :, j], pj, lg[:, 0, :, :], ALU.is_equal)
                v.drain()
                v.tensor_tensor(cmp_[:, 2, :, :, :], cmp_[:, 1, :, :, :], before[:, :, :, :], ALU.mult)
                v.tensor_tensor(lg[:, 3, :, :], lg[:, 0, :, :], over(r1[:, 3, :]), ALU.subtract).then_inc(s_lge, 1)
                v.drain()
                v.tensor_tensor(cmp_[:, 1, :, :, :], cmp_[:, 0, :, :, :], cmp_[:, 2, :, :, :], ALU.add)
                v.drain()
                v.tensor_reduce(lg[:, 5, :, :], cmp_[:, 1, :, :, :], AX.X, ALU.add)
                v.drain()
                dve.wait_ge(s_lgx, 2 * b + 2)
                v.scalar_tensor_tensor(lg[:, 1, :, :], lg[:, 5, :, :], 2.0, lg[:, 4, :, :], ALU.is_lt, ALU.mult)
                v.drain()
                v.tensor_reduce(r1[:, 4, :], lg[:, 1, :, :], AX.X, ALU.add)
                v.drain()
                v.reciprocal(r1[:, 5, :], r1[:, 4, :])
                v.drain()
                v.tensor_tensor(lg[:, 5, :, :], lg[:, 1, :, :], over(r1[:, 5, :]), ALU.mult).then_inc(s_comb, 1)
                for t in range(TC):
                    v.drain()
                    dve.wait_ge(s_y, 20 * b + t + 5)
                    v.tensor_tensor(x2[:, t, :], ps[:, SA + t, :], x2[:, t, :], ALU.add).then_inc(s_ye, 1)
                for e in range(E):
                    for t in range(TC):
                        v.drain()
                        dve.wait_ge(s_y, 20 * b + 4 * e + t + 9)
                        v.scalar_tensor_tensor(x2[:, t, :], ps[:, SA + t, :], lg[:, 5, t, e:e + 1], x2[:, t, :],
                                               ALU.mult, ALU.add).then_inc(s_ye, 1)
                layer_norm(4 * b + 4, x2, xn).then_inc(s_fin, 1)
                v.drain()

        @block.tensor
        def _(pe):
            mm = nc.tensor.matmul
            tr = nc.tensor.transpose
            pe.wait_ge(s_const, 128)
            pe.sem_inc(s_QK, 8)
            pe.sem_inc(s_V, 4)
            pe.sem_inc(s_O, 4)
            pe.sem_inc(s_h1, 4)
            pe.sem_inc(s_y, 4)

            def transposed(b, which):
                pe.wait_ge(s_xn, 2 * b + which + 1)
                for c in range(C):
                    for t in range(TC):
                        ins = tr(ps[:, PJ + c, t * P:(t + 1) * P], xn[:, t, c * P:(c + 1) * P], ident[:, :])
                    ins.then_inc(s_nT, 1)

            def project_qk(G, hh):
                for a in range(2):
                    bank = PJ + 2 * (hh % 2) + a
                    if hh < 2:
                        pe.wait_ge(s_Oe, 4 * G + 2 * hh + a + 1)
                    else:
                        pe.wait_ge(s_Ve, 4 * G + 2 * (hh - 2) + a + 1)
                    if hh == 0:
                        pe.wait_ge(s_w[a], 16 * G + 16)
                    for k in range(C):
                        ins = mm(ps[:, bank, :], wa[:, a, k, hh * P:(hh + 1) * P], xT[:, k, :], start=(k == 0),
                                 stop=(k == C - 1))
                    ins.then_inc(s_QK, 1)

            def scores(n, hh):
                pe.wait_ge(s_rope, 2 * n + 4)
                q, k = qk[:, hh % 2, 0, :], qk[:, hh % 2, 1, :]
                for t, dst in enumerate([ps[:, SA, 0:P], ps[:, SA, P:3 * P], ps[:, SB, 0:3 * P], ps[:, SC, 0:4 * P]]):
                    mm(dst, q[:, t * P:(t + 1) * P], k[:, 0:(t + 1) * P], start=True, stop=True).then_inc(s_S, 1)

            def values(G):
                pe.wait_ge(s_w[2], 16 * G + 16)
                for t in range(TC):
                    pe.wait_ge(s_rope, 8 * G + t + 3)
                    for k in range(C):
                        ins = mm(ps[:, PJ + t, :], xT[:, k, t * P:(t + 1) * P], wa[:, 2, k, :], start=(k == 0),
                                 stop=(k == C - 1))
                    ins.then_inc(s_V, 1)

            def transpose_probs(n):
                pe.wait_ge(s_Pn, n + 1)
                for t in range(TC):
                    ins = tr(ps[:, SA, t * P:(t + 1) * P], Pr[:, t, 0:P], ident[:, :])
                ins.then_inc(s_T, 1)
                for t in range(1, TC):
                    tr(ps[:, SB, (t - 1) * P:t * P], Pr[:, t, P:2 * P], ident[:, :])
                tr(ps[:, SB, 3 * P:T], Pr[:, 3, 3 * P:T], ident[:, :]).then_inc(s_T, 1)
                for t in range(2, TC):
                    ins = tr(ps[:, SC, (t - 2) * P:(t - 1) * P], Pr[:, t, 2 * P:3 * P], ident[:, :])
                ins.then_inc(s_T, 1)

            def weigh_values(G, n, hh):
                if hh == 0:
                    pe.wait_ge(s_Ve, 4 * G + 4)
                pe.wait_ge(s_OT, n + 1)
                for i, j in enumerate((0, 1, 3, 2)):
                    pe.wait_ge(s_PT, 3 * n + (1, 2, 2, 3)[i])
                    ins = mm(ps[:, PV, j * P:T], Vg[:, j, hh * P:(hh + 1) * P], PT[:, j, j * P:T], start=(i == 0),
                             stop=(i == 3), skip_group_check=True)
                ins.then_inc(s_PV, 1)

            def project_out(G, heads):
                for t in range(TC):
                    if heads[0] == 0:
                        pe.wait_ge(s_rope, 8 * G + t + 7)
                    for hh in heads:
                        ins = mm(ps[:, PJ + t, :], OT[:, hh, t * P:(t + 1) * P], wa[:, 3, hh, :], start=(hh == 0),
                                 stop=(hh == GH - 1), skip_group_check=True)
                    if heads[-1] == GH - 1:
                        ins.then_inc(s_O, 1)

            with pe.Fori(0, B) as b:
                pe.wait_ge(s_xA, 4 * b + 4)
                for t in range(TC):
                    for m in range(TC):
                        ins = tr(ps[:, PJ + t, m * P:(m + 1) * P], sx[:, m, t * P:(t + 1) * P], ident[:, :])
                    ins.then_inc(s_xAT, 1)
                transposed(b, 0)
                with pe.Fori(0, NG) as g:
                    G = b * NG + g
                    pe.wait_ge(s_nTe, 8 * b + 4)
                    project_qk(G, 0)
                    project_qk(G, 1)
                    for hh in range(GH):
                        n = 4 * G + hh
                        scores(n, hh)
                        if hh == 0:
                            values(G)
                        elif hh < 3:
                            project_qk(G, hh + 1)
                        else:
                            pe.wait_ge(s_w[3], 16 * G + 16)
                            pe.wait_ge(s_OT, n + 1)
                            project_out(G, range(3))
                        transpose_probs(n)
                        weigh_values(G, n, hh)
                    pe.wait_ge(s_OT, 4 * G + 5)
                    project_out(G, [3])
                transposed(b, 1)
                pe.wait_ge(s_nTe, 8 * b + 8)
                for t in range(TC):
                    for k in range(C):
                        ins = mm(ps[:, SA, t * E:(t + 1) * E], xT[:, k, t * P:(t + 1) * P], wg[:, k, :],
                                 start=(k == 0), stop=(k == C - 1))
                ins.then_inc(s_lg, 1)

                def expert_in(e):
                    pe.wait_ge(s_we[0], 64 * b + 16 * e + 16)
                    for i in range(C):
                        pe.wait_ge(s_gel, 16 * b + 4 * e + i + 1)
                        for k in range(C):
                            ins = mm(ps[:, PJ + i, :], we[:, 0, k, i * P:(i + 1) * P], xT[:, k, :], start=(k == 0),
                                     stop=(k == C - 1))
                        ins.then_inc(s_h1, 1)

                def expert_out(e):
                    pe.wait_ge(s_we[1], 64 * b + 16 * e + 16)
                    pe.wait_ge(s_gel, 16 * b + 4 * e + 8)
                    for t in range(TC):
                        pe.wait_ge(s_ye, 20 * b + 4 * e + t + 5)
                        for i in range(C):
                            ins = mm(ps[:, SA + t, :], hm[:, e % 2, i, t * P:(t + 1) * P], we[:, 1, i, :],
                                     start=(i == 0), stop=(i == C - 1))
                        ins.then_inc(s_y, 1)

                expert_in(0)
                pe.wait_ge(s_comb, b + 1)
                for t in range(TC):
                    ins = tr(ps[0:E, SB, t * P:(t + 1) * P], lg[:, 5, t, :], ident[:, :])
                ins.then_inc(s_cT, 1)
                pe.wait_ge(s_cTe, b + 1)
                for t in range(TC):
                    mm(ps[:, SA + t, :], combT[:, t * P:(t + 1) * P], be2[:, :], start=True, stop=True).then_inc(s_y, 1)
                expert_out(0)
                for e in range(1, E):
                    expert_in(e)
                    expert_out(e)


def decoder(nc, dram, out):
    x1_d = nc.dram_tensor("x1_scratch", (B, P, TC, D), F32, kind="Internal").ap()
    sim_d = nc.dram_tensor("sim_scratch", (B, P, TC, T), F32, kind="Internal").ap()
    block_a(nc, dram, x1_d, sim_d)
    block_c(nc, dram, x1_d, sim_d, out)


def rope_tables():
    f = np.float32
    inv = f(1.0) / np.power(f(10000.0), np.arange(0, P, 2, dtype=f) / f(P)).astype(f)
    ang = (np.arange(T, dtype=f)[:, None] * inv[None, :]).astype(f)
    ang = np.concatenate([ang, ang], 1).T
    cos, sin = np.cos(ang).astype(f), np.sin(ang).astype(f)
    sin[:P // 2] *= -1
    s = f(P ** -0.5)
    return np.ascontiguousarray(np.stack([cos * s, sin * s, cos, sin], 1))


def kernel(**inputs):
    from concourse import bacc
    from concourse.bass_utils import run_bass_kernel_spmd

    a = {k: np.asarray(v) for k, v in inputs.items()}

    def rows(w):
        return w.reshape(-1, P, w.shape[-1]).transpose(1, 0, 2)

    def feat(w):
        return w.reshape(-1, P).T

    def tokens(x):
        return x.reshape(B, TC, P, -1).transpose(0, 2, 1, 3)

    f = "L0_ffn_"
    r = "L0_attn_"
    vec = np.concatenate(
        [feat(a[r + "time_mix_" + n]) for n in ("key", "value", "receptance")]
        + [feat(a[r + "time_decay"]), feat(a[r + "time_first"])]
        + [feat(a[f + n]) for n in ("bq", "bk", "bv", "ln1_w", "ln1_b", "ln2_w", "ln2_b", "be1")]
        + [np.broadcast_to(a["L0_xattn_gamma_raw"].reshape(1, 1), (P, 1))], axis=1)
    xT = a["x"].reshape(B, T, C, P).transpose(0, 3, 2, 1)
    groups = (C, P, NG, GH * P)
    before = np.broadcast_to((np.arange(E)[None, :] < np.arange(E)[:, None]).astype(np.float32), (P, TC, E, E))
    q = np.arange(P)
    arrays = {
        "vec": vec,
        "wqkT": np.stack([a["L0_xattn_Wq"].T, a["L0_xattn_Wk"].T], 1),
        "W": np.stack([rows(a[r + n]) for n in ("Wk", "Wv", "Wr", "Wo")]),
        "x": tokens(a["x"]),
        "xT": np.pad(xT, ((0, 0), (0, 0), (0, 0), (1, 0))),
        "cT": a["ctx_512"].transpose(0, 2, 1),
        "ident": np.eye(P, dtype=np.float32),
        "rope": rope_tables(),
        "causal": np.where(q[None, :] > q[:, None], np.float32(NEG), np.float32(0)),
        "before": before,
        "bo": np.broadcast_to(a[f + "bo"], (P, D)),
        "wg": rows(a[f + "w_gate"]),
        "be2": a[f + "be2"],
        "wq": a[f + "wq"].reshape(groups).transpose(2, 1, 0, 3),
        "wk": a[f + "wk"].reshape(groups).transpose(2, 1, 0, 3),
        "wv": a[f + "wv"].reshape(groups).transpose(2, 1, 0, 3),
        "wo": a[f + "wo"].reshape(NG, GH, P, D).transpose(0, 2, 1, 3),
        "we1": np.stack([rows(w) for w in a[f + "we1"]]),
        "we2": np.stack([rows(w) for w in a[f + "we2"]]),
    }
    arrays = {k: np.ascontiguousarray(w) for k, w in arrays.items()}
    nc = bacc.Bacc("TRN2", target_bir_lowering=False, num_devices=1)
    dram = {k: nc.dram_tensor("in_" + k, w.shape, mybir.dt.from_np(w.dtype), kind="ExternalInput").ap()
            for k, w in arrays.items()}
    out = nc.dram_tensor("out_x", (B, P, TC, D), F32, kind="ExternalOutput").ap()
    decoder(nc, dram, out)
    res = run_bass_kernel_spmd(nc, [{"in_" + k: w for k, w in arrays.items()}], core_ids=[0])
    y = res.results[0]["out_x"]
    return y.transpose(0, 2, 1, 3).reshape(B, T, D)
```

```python
from contextlib import ExitStack

import numpy as np

import concourse.bass as bass
from concourse import mybir

F32 = mybir.dt.float32
F32R = mybir.dt.float32r
ALU = mybir.AluOpType
ACT = mybir.ActivationFunctionType
AX = mybir.AxisListType

P = 128
B, T, D = 4, 512, 512
C = D // P
TC = T // P
HEADS = 16
GH = 4
NG = HEADS // GH
E = 4
DM = 128
XHEADS = 4
TOPK = int(T * 0.3)
ROUNDS = -(-TOPK // 8)
RPG = ROUNDS // NG
KTH = (TOPK - 1) % 8
assert ROUNDS == RPG * NG
EPS = 1e-5
SIM_SCALE = float(1.0 / (np.sqrt(np.float32(DM // XHEADS)) * XHEADS))
NEG = -1e30
MX0 = -1e38

SETS = NG + E // 2
MATS = 4 * SETS
SLOTS = (2, 0, 1, 3)
COL = {}
_n = 0
for _name, _w in [("mix", 12), ("decay", 4), ("first", 4), ("bq", 16), ("bk", 16), ("bv", 16),
                  ("ln1w", 4), ("ln1b", 4), ("ln2w", 4), ("ln2b", 4), ("be1", 16), ("gamma", 1)]:
    COL[_name] = _n
    _n += _w
NCOL = _n


def take_largest(nc, m8, tk, tiles, rounds):
    v = nc.vector
    for _ in range(rounds):
        for t in tiles:
            v.max(m8[:, t, :], tk[:, t, :])
        v.drain()
        for t in tiles:
            v.match_replace(tk[:, t, :], m8[:, t, :], tk[:, t, :], NEG)
        v.drain()


def block_a(nc, dram, x1_d, sim_d, m8):
    with ExitStack() as ctx:
        def sb(name, shape):
            return ctx.enter_context(nc.sbuf_tensor(name, shape, F32))

        def sem(name):
            return ctx.enter_context(nc.semaphore(name))

        W = sb("W", [P, 4, C, D])
        vec = sb("vecA", [P, NCOL])
        omm = sb("omm", [P, 12])
        td = sb("td", [P, C])
        wqk = sb("wqk", [P, 2, DM])
        xT = sb("xT", [P, C, T + 1])
        xr = sb("xr", [P, TC, D])
        cT = sb("cT", [P, T])
        tmp = sb("tmp", [P, 2, 2, T])
        mk = sb("mk", [P, 3, C, T])
        qk = sb("qkA", [P, 2, T])
        sim = sb("simA", [P, TC, T])
        Mx = sb("Mx", [P, T + 1])
        dg = sb("dg", [P, 2, 2, T])
        rr = sb("rr", [P, 2, 2, T])
        ee = sb("ee", [P, 2, 4, T])
        Dn = sb("Dn", [P, 2, T + 1])
        Nm = sb("Nm", [P, 2, T + 1])
        vs = sb("vs", [P, 2, T])
        th = sb("th", [P, 2, T])
        ev = sb("ev", [P, 2, T])
        p2 = sb("p2", [P, 2, T])
        q1 = sb("q1", [P, 2, T])
        p1 = sb("p1", [P, 2, T])
        den = sb("den", [P, T])
        num = sb("num", [P, T])
        rec = sb("rec", [P, T])
        num2 = sb("num2", [P, T])
        rw = sb("rw", [P, C, T])
        z = sb("z", [P, TC, D])
        st = sb("stA", [P, TC, 6])
        mv = sb("mvA", [P, TC, 2])
        var = sb("varA", [P, TC])
        mhalf = sb("mhalfA", [P, TC])
        rstd = sb("rstdA", [P, TC])
        x1 = sb("x1A", [P, TC, D])
        tk = sb("tkA", [P, TC, T])
        ps = ctx.enter_context(nc.psum_tensor("psA", [P, 8, 512], F32))
        E1, E2S, E2, E1S = 0, 1, 2, 3
        Y = 6

        s_const = sem("a_const")
        s_xT = sem("a_xT")
        s_xr = sem("a_xr")
        s_cT = sem("a_cT")
        s_pre = sem("a_pre")
        s_half = sem("a_half")
        s_sh = sem("a_sh")
        s_mix = sem("a_mix")
        s_proj = sem("a_proj")
        s_dg = sem("a_dg")
        s_vt = sem("a_vt")
        s_e = sem("a_e")
        s_ev = sem("a_ev")
        s_scan = sem("a_scan")
        s_pq = sem("a_pq")
        s_rw = sem("a_rw")
        s_sps = sem("a_sps")
        s_sev = sem("a_sev")
        s_y = sem("a_y")
        s_z = sem("a_z")
        s_var = sem("a_var")
        s_rstd = sem("a_rstd")
        s_x1 = sem("a_x1")
        s_x1o = sem("a_x1o")
        s_simo = sem("a_simo")

        block = ctx.enter_context(nc.Block())

        @block.sync
        def _(sp):
            sp.dma_start(xT[:, :, :], dram["xT"][0]).then_inc(s_xT, 16)
            sp.dma_start(vec[:, :], dram["vec"]).then_inc(s_const, 16)
            sp.dma_start(wqk[:, :, :], dram["wqkT"]).then_inc(s_const, 16)
            for i in range(4):
                sp.dma_start(W[:, i, :, :], dram["W"][i]).then_inc(s_const, 16)
            sp.sem_inc(s_x1o, 16)
            sp.sem_inc(s_simo, 16)
            with sp.Fori(0, B) as b:
                sp.wait_ge(s_sh, 12 * b + 12)
                sp.dma_start(xT[:, :, :], dram["xT"][(b + 1) % B]).then_inc(s_xT, 16)
                sp.wait_ge(s_sev, 6 * b + 12)
                sp.dma_start(sim_d[b], sim[:, :, :]).then_inc(s_simo, 16)
                sp.wait_ge(s_x1, b + 1)
                sp.dma_start(x1_d[b], x1[:, :, :]).then_inc(s_x1o, 16)
            sp.wait_ge(s_simo, 16 * B + 16)
            sp.wait_ge(s_x1o, 16 * B + 16)
            sp.wait_ge(s_xT, 16 * B + 16)

        @block.gpsimd
        def _(pool):
            nc.gpsimd.memset(mhalf[:, :], -0.5).then_inc(s_half, 1)
            pool.wait_ge(s_half, 1)
            pool.dma_start(cT[:, :], dram["cT"][0]).then_inc(s_cT, 16)
            pool.dma_start(xr[:, :, :], dram["x"][0]).then_inc(s_xr, 16)

            def ev_products(b, c):
                i = c % 2
                pool.wait_ge(s_vt, 4 * b + c + 3)
                pool.wait_ge(s_e, 4 * b + c + 1)
                nc.gpsimd.tensor_tensor(ev[:, i, :], ee[:, i, E2S, :], vs[:, i, :], ALU.mult).then_inc(s_ev, 1)
                nc.gpsimd.tensor_tensor(p2[:, i, :], ee[:, i, E2, :], vs[:, i, :], ALU.mult).then_inc(s_ev, 1)

            def sum_products(b, c):
                i = c % 2
                pool.wait_ge(s_scan, 4 * b + c + 1)
                nc.gpsimd.tensor_tensor(q1[:, i, :], ee[:, i, E1, :], Dn[:, i, 0:T], ALU.mult).then_inc(s_pq, 1)
                nc.gpsimd.tensor_tensor(p1[:, i, :], ee[:, i, E1, :], Nm[:, i, 0:T], ALU.mult).then_inc(s_pq, 1)

            def mixes(bm, c):
                for m in range(3):
                    j = 3 * c + m
                    pool.wait_ge(s_sh, 12 * bm + j + 1)
                    nc.gpsimd.tensor_tensor(mk[:, m, c, :], tmp[:, j % 2, 0, :], tmp[:, j % 2, 1, :],
                                            ALU.add).then_inc(s_mix, 1)

            pool.sem_inc(s_mix, 2)
            for c in range(C):
                mixes(0, c)
            with pool.Fori(0, B) as b:
                for c in range(C):
                    ev_products(b, c)
                    if c >= 1:
                        sum_products(b, c - 1)
                pool.wait_ge(s_proj, 12 * b + 12)
                mixes(b + 1, 0)
                sum_products(b, C - 1)
                for c in range(1, C):
                    mixes(b + 1, c)
                pool.wait_ge(s_sps, 6 * b + 12)
                pool.dma_start(cT[:, :], dram["cT"][(b + 1) % B]).then_inc(s_cT, 16)
                pool.wait_ge(s_var, b + 1)
                nc.gpsimd.tensor_tensor(rstd[:, :], var[:, :], mhalf[:, :], ALU.pow).then_inc(s_rstd, 1)
                pool.wait_ge(s_z, 4 * b + 8)
                pool.dma_start(xr[:, :, :], dram["x"][(b + 1) % B]).then_inc(s_xr, 16)
            pool.wait_ge(s_cT, 16 * B + 16)
            pool.wait_ge(s_xr, 16 * B + 16)

        @block.scalar
        def _(act):
            act.wait_ge(s_const, 96)
            nc.scalar.activation(td[:, :], vec[:, COL["decay"]:COL["decay"] + C], ACT.Exp).then_inc(s_pre, 1)
            act.wait_ge(s_pre, 5)
            act.sem_inc(s_vt, 2)

            def mix_products(bm, c):
                for m in range(3):
                    j = 3 * c + m
                    act.wait_ge(s_mix, 12 * bm + j + 1)
                    nc.scalar.mul(tmp[:, j % 2, 0, :], xT[:, c, 1:T + 1],
                                  vec[:, COL["mix"] + 4 * m + c:COL["mix"] + 4 * m + c + 1])
                    nc.scalar.mul(tmp[:, j % 2, 1, :], xT[:, c, 0:T],
                                  omm[:, 4 * m + c:4 * m + c + 1]).then_inc(s_sh, 1)

            def chunk(b, c):
                i = c % 2
                act.wait_ge(s_rw, 4 * b + c + 3)
                act.wait_ge(s_proj, 12 * b + 3 * c + 2)
                nc.scalar.copy(vs[:, i, :], ps[:, 3 * i + 1, :])
                act.wait_ge(s_proj, 12 * b + 3 * c + 3)
                nc.scalar.activation(th[:, i, :], ps[:, 3 * i + 2, :], ACT.Tanh, scale=0.5).then_inc(s_vt, 1)
                act.drain()
                act.wait_ge(s_dg, 4 * b + c + 3)
                nc.scalar.activation(rr[:, 0, :, :], dg[:, i, :, :], ACT.Relu)
                nc.scalar.activation(rr[:, 1, :, :], dg[:, i, :, :], ACT.Relu, scale=-1.0)
                act.drain()
                nc.scalar.activation(ee[:, i, :, :].rearrange("p a t -> p (a t)"),
                                     rr[:, :, :, :].rearrange("p a c t -> p (a c t)"), ACT.Exp,
                                     scale=-1.0).then_inc(s_e, 1)

            act.wait_ge(s_xT, 16)
            for c in range(C):
                mix_products(0, c)
            for j in range(2):
                act.wait_ge(s_sps, j + 1)
                nc.scalar.copy(qk[:, j, :], ps[:, Y + j, :]).then_inc(s_sev, 1)
            for t in range(TC):
                act.wait_ge(s_sps, t + 3)
                nc.scalar.mul(tk[:, t, :], ps[:, Y + t % 2, :], SIM_SCALE).then_inc(s_sev, 1)
            with act.Fori(0, B) as b:
                chunk(b, 0)
                chunk(b, 1)
                act.wait_ge(s_simo, 16 * b + 16)
                for j in range(2):
                    act.wait_ge(s_sps, 6 * b + j + 7)
                    nc.scalar.copy(qk[:, j, :], ps[:, Y + j, :]).then_inc(s_sev, 1)
                for t in range(TC):
                    act.wait_ge(s_sps, 6 * b + t + 9)
                    nc.scalar.mul(sim[:, t, :], ps[:, Y + t % 2, :], SIM_SCALE).then_inc(s_sev, 1)
                chunk(b, 2)
                chunk(b, 3)
                act.wait_ge(s_xT, 16 * b + 32)
                for c in range(C):
                    mix_products(b + 1, c)

        @block.vector
        def _(dve):
            v = nc.vector
            v.memset(Mx[:, 0:1], MX0).then_inc(s_pre, 1)
            v.memset(Dn[:, :, 0:1], 0.0).then_inc(s_pre, 1)
            v.memset(Nm[:, :, 0:1], 0.0).then_inc(s_pre, 1)
            dve.wait_ge(s_const, 96)
            v.tensor_scalar(omm[:, :], vec[:, 0:12], -1.0, 1.0, ALU.mult, ALU.add).then_inc(s_pre, 1)
            dve.wait_ge(s_pre, 5)
            v.tensor_scalar(td[:, :], td[:, :], -1.0, None, ALU.mult)
            dve.sem_inc(s_dg, 2)
            dve.sem_inc(s_rw, 4)
            dve.sem_inc(s_z, 4)

            def exponents(b, c):
                k = ps[:, 3 * (c % 2), :]
                v.drain()
                dve.wait_ge(s_proj, 12 * b + 3 * c + 1)
                v.tensor_tensor_scan(Mx[:, 1:T + 1], td[:, c:c + 1].to_broadcast([P, T]), k, MX0, ALU.add, ALU.max)
                v.drain()
                v.scalar_tensor_tensor(dg[:, c % 2, 0, :], k, vec[:, COL["first"] + c:COL["first"] + c + 1],
                                       Mx[:, 0:T], ALU.add, ALU.subtract)
                v.scalar_tensor_tensor(dg[:, c % 2, 1, :], Mx[:, 0:T], td[:, c:c + 1], k, ALU.add,
                                       ALU.subtract).then_inc(s_dg, 1)

            def sums(b, c):
                i = c % 2
                dve.wait_ge(s_e, 4 * b + c + 1)
                v.tensor_tensor_scan(Dn[:, i, 1:T + 1], ee[:, i, E1S, :], ee[:, i, E2S, :], 0.0, ALU.mult, ALU.add)
                dve.wait_ge(s_ev, 8 * b + 2 * c + 1)
                v.tensor_tensor_scan(Nm[:, i, 1:T + 1], ee[:, i, E1S, :], ev[:, i, :], 0.0, ALU.mult,
                                     ALU.add).then_inc(s_scan, 1)

            def outputs(b, c):
                i = c % 2
                v.drain()
                dve.wait_ge(s_pq, 8 * b + 2 * c + 2)
                v.tensor_tensor(den[:, :], q1[:, i, :], ee[:, i, E2, :], ALU.add)
                v.tensor_tensor(num[:, :], p1[:, i, :], p2[:, i, :], ALU.add)
                v.drain()
                v.reciprocal(rec[:, :], den[:, :])
                v.scalar_tensor_tensor(num2[:, :], th[:, i, :], 1.0, num[:, :], ALU.add, ALU.mult)
                v.drain()
                v.scalar_tensor_tensor(rw[:, c, :], num2[:, :], 0.5, rec[:, :], ALU.mult,
                                       ALU.mult).then_inc(s_rw, 1)

            def search():
                take_largest(nc, m8, tk, range(TC), 1)

            dve.wait_ge(s_sev, 6)
            with dve.Fori(0, B) as b:
                search()
                exponents(b, 0)
                search()
                exponents(b, 1)
                sums(b, 0)
                exponents(b, 2)
                search()
                outputs(b, 0)
                sums(b, 1)
                exponents(b, 3)
                outputs(b, 1)
                sums(b, 2)
                search()
                outputs(b, 2)
                sums(b, 3)
                outputs(b, 3)
                search()
                dve.wait_ge(s_xr, 16 * b + 16)
                for t in range(TC):
                    dve.wait_ge(s_y, 4 * b + t + 1)
                    v.tensor_tensor(z[:, t, :], ps[:, Y + t % 2, :], xr[:, t, :], ALU.add).then_inc(s_z, 1)
                    v.drain()
                    v.bn_stats(st[:, t, :], z[:, t, :])
                v.drain()
                for t in range(TC):
                    v.bn_aggr(mv[:, t, :], st[:, t, :])
                v.drain()
                v.tensor_scalar(var[:, :], mv[:, :, 1], EPS, None, ALU.add).then_inc(s_var, 1)
                dve.wait_ge(s_x1o, 16 * b + 16)
                dve.wait_ge(s_rstd, b + 1)
                for t in range(TC):
                    ins = v.tensor_scalar(x1[:, t, :], z[:, t, :], mv[:, t, 0:1], rstd[:, t:t + 1],
                                          ALU.subtract, ALU.mult)
                ins.then_inc(s_x1, 1)

        @block.tensor
        def _(pe):
            mm = nc.tensor.matmul
            pe.wait_ge(s_const, 96)

            def project(b, c):
                pe.wait_ge(s_dg, 4 * b + c + 1)
                pe.wait_ge(s_vt, 4 * b + c + 1)
                if c == 0:
                    pe.wait_ge(s_mix, 12 * b + 14)
                for m in range(3):
                    for k in range(C):
                        ins = mm(ps[:, 3 * (c % 2) + m, :], W[:, m, k, c * P:(c + 1) * P], mk[:, m, k, :],
                                 start=(k == 0), stop=(k == C - 1))
                    ins.then_inc(s_proj, 1)

            def similarities(n):
                for j in range(2):
                    mm(ps[:, Y + j, :], wqk[:, j, :], cT[:, :], start=True, stop=True).then_inc(s_sps, 1)
                pe.wait_ge(s_sev, n + 2)
                for t in range(TC):
                    if t >= 2:
                        pe.wait_ge(s_sev, n + t + 1)
                    mm(ps[:, Y + t % 2, :], qk[:, 0, t * P:(t + 1) * P], qk[:, 1, :], start=True,
                       stop=True).then_inc(s_sps, 1)

            pe.wait_ge(s_cT, 16)
            similarities(0)
            with pe.Fori(0, B) as b:
                project(b, 0)
                project(b, 1)
                pe.wait_ge(s_cT, 16 * b + 16)
                pe.wait_ge(s_sev, 6 * b + 6)
                pe.wait_ge(s_z, 4 * b + 4)
                similarities(6 * b + 6)
                project(b, 2)
                project(b, 3)
                pe.wait_ge(s_sev, 6 * b + 12)
                pe.wait_ge(s_rw, 4 * b + 8)
                for t in range(TC):
                    if t >= 2:
                        pe.wait_ge(s_z, 4 * b + t + 3)
                    for c in range(C):
                        ins = mm(ps[:, Y + t % 2, :], rw[:, c, t * P:(t + 1) * P], W[:, 3, c, :],
                                 start=(c == 0), stop=(c == C - 1))
                    ins.then_inc(s_y, 1)


def block_c(nc, dram, x1_d, sim_d, m8, out):
    with ExitStack() as ctx:
        def sb(name, shape, dt=F32):
            return ctx.enter_context(nc.sbuf_tensor(name, shape, dt))

        def sem(name):
            return ctx.enter_context(nc.semaphore(name))

        vec = sb("vec", [P, NCOL])
        ident = sb("ident", [P, P])
        rope = sb("rope", [P, 4, T])
        causal = sb("causal", [P, P], F32R)
        identr = sb("identr", [P, P], F32R)
        before = sb("before", [P, TC, E, E])
        bo = sb("bo", [P, D])
        wg = sb("wg", [P, C, E])
        be2 = sb("be2", [E, D])
        gam = sb("gam", [P, 4])
        mhalf = sb("mhalf", [P, TC])
        ws = sb("ws", [P, 2, C * D])
        wh = sb("wh", [P, 4, C, D], F32R)
        wl = sb("wl", [P, 4, C, D], F32R)
        wgh = sb("wgh", [P, C, E], F32R)
        wgl = sb("wgl", [P, C, E], F32R)
        tk = sb("tk", [P, TC, T])
        thr = sb("thr", [P, TC])
        x2 = sb("x2", [P, TC, D])
        xn = sb("xn", [P, TC, D])
        xf = sb("xf", [P, 2, T])
        xh = sb("xh", [P, C, T], F32R)
        xl = sb("xl", [P, C, T], F32R)
        h = sb("h", [P, TC, D])
        st = sb("st", [P, TC, 6])
        mv = sb("mv", [P, TC, 2])
        var = sb("var", [P, TC])
        rstd = sb("rstd", [P, TC])
        sh = sb("sh", [P, 2, T])
        rc = sb("rc", [P, 2, T])
        qk = sb("qk", [P, 2, 2, T])
        Vg = sb("Vg", [P, TC, GH * P])
        Pr = sb("Pr", [P, TC, T])
        sx = Pr
        x1 = Vg
        nmax = sb("nmax", [P, TC])
        rsum = sb("rsum", [P, TC])
        rinv = sb("rinv", [P, TC])
        PT = sb("PT", [P, TC, T])
        tx = PT
        of = sb("of", [P, 2, T])
        oh = sb("oh", [P, GH, T], F32R)
        ol = sb("ol", [P, GH, T], F32R)
        lg = sb("lg", [P, 6, TC, E])
        r1 = sb("r1", [P, 6, TC])
        cmp_ = rc[:, 1, 0:3 * TC * E * E].rearrange("p (a t e j) -> p a t e j", a=3, t=TC, e=E)
        combT = rc[0:E, 0, :]
        ps = ctx.enter_context(nc.psum_tensor("ps", [P, 8, 512], F32))
        PJ, SA, SB, SC, PV = 0, 4, 5, 6, 7

        s_const = sem("c_const")
        s_pre = sem("c_pre")
        s_tanh = sem("c_tanh")
        s_half = sem("c_half")
        s_tkin = sem("c_tkin")
        s_tkdone = sem("c_tkdone")
        s_xin = sem("c_xin")
        s_xth = sem("c_xth")
        s_xA = sem("c_xA")
        s_xAT = sem("c_xAT")
        s_xATe = sem("c_xATe")
        s_var = sem("c_var")
        s_rstd = sem("c_rstd")
        s_xn = sem("c_xn")
        s_nT = sem("c_nT")
        s_nTe = sem("c_nTe")
        s_ws = [sem(f"c_ws{i}") for i in range(2)]
        s_wh = sem("c_wh")
        s_split = sem("c_split")
        s_xs = sem("c_xs")
        s_Oh = sem("c_Oh")
        s_Os = sem("c_Os")
        s_hs = sem("c_hs")
        s_QK = sem("c_QK")
        s_V = sem("c_V")
        s_Ve = sem("c_Ve")
        s_sh = sem("c_sh")
        s_rs = sem("c_rs")
        s_rope = sem("c_rope")
        s_S = sem("c_S")
        s_nm = sem("c_nm")
        s_P = sem("c_P")
        s_Pn = sem("c_Pn")
        s_T = sem("c_T")
        s_PT = sem("c_PT")
        s_PV = sem("c_PV")
        s_OT = sem("c_OT")
        s_O = sem("c_O")
        s_Oe = sem("c_Oe")
        s_lg = sem("c_lg")
        s_lge = sem("c_lge")
        s_lgx = sem("c_lgx")
        s_comb = sem("c_comb")
        s_cT = sem("c_cT")
        s_cTe = sem("c_cTe")
        s_h1 = sem("c_h1")
        s_gel = sem("c_gel")
        s_y = sem("c_y")
        s_ye = sem("c_ye")
        s_fin = sem("c_fin")
        s_out = sem("c_out")

        block = ctx.enter_context(nc.Block())

        @block.sync
        def _(sp):
            sp.dma_start(sx[:, :, :], sim_d[0]).then_inc(s_xin, 16)
            sp.dma_start(x1[:, :, :], x1_d[0]).then_inc(s_xin, 16)
            for dst, name in [(vec[:, :], "vec"), (ident[:, :], "ident"), (rope[:, :, :], "rope"),
                              (xf[:, 0, 0:P], "causal"), (before[:, :, :, :], "before"), (bo[:, :], "bo"),
                              (wg[:, :, :], "wg"), (be2[:, :], "be2")]:
                sp.dma_start(dst, dram[name]).then_inc(s_const, 16)

            def load(b, st, i):
                sp.wait_ge(s_split, MATS * b + 4 * st + i + 1)
                sp.dma_start(ws[:, i % 2, :], dram["wset"][st, i]).then_inc(s_ws[i % 2], 16)

            sp.dma_start(tk[:, :, :], sim_d[1]).then_inc(s_tkin, 16)
            with sp.Fori(0, B) as b:
                with sp.Fori(0, NG) as g:
                    for i in range(4):
                        load(b, g, i)
                for i in range(4):
                    load(b, NG, i)
                sp.wait_ge(s_PV, 16 * b + 16)
                sp.dma_start(sx[:, :, :], sim_d[(b + 1) % B]).then_inc(s_xin, 16)
                sp.dma_start(x1[:, :, :], x1_d[(b + 1) % B]).then_inc(s_xin, 16)
                sp.wait_ge(s_tkdone, b + 2)
                sp.dma_start(tk[:, :, :], sim_d[(b + 2) % B]).then_inc(s_tkin, 16)
                for i in range(4):
                    load(b, NG + 1, i)
            for i in range(4):
                load(B, 0, i)
            sp.wait_ge(s_tkin, 16 * B + 16)

        @block.gpsimd
        def _(pool):
            nc.gpsimd.memset(mhalf[:, :], -0.5).then_inc(s_half, 1)
            pool.wait_ge(s_half, 1)
            pool.wait_ge(s_const, 128)
            pool.sem_inc(s_split, 2)
            pool.sem_inc(s_Os, 2)

            def root(n):
                pool.wait_ge(s_var, n)
                nc.gpsimd.tensor_tensor(rstd[:, :], var[:, :], mhalf[:, :], ALU.pow).then_inc(s_rstd, 1)

            def sines(n, a):
                pool.wait_ge(s_sh, 2 * n + a + 1)
                nc.gpsimd.tensor_tensor(sh[:, a, :], sh[:, a, :], rope[:, 2 * a + 1, :], ALU.mult).then_inc(s_rs, 1)


            def weight_lo(K, i):
                pool.wait_ge(s_wh, K + 1)
                nc.gpsimd.tensor_tensor(wl[:, SLOTS[i], :, :].rearrange("p c n -> p (c n)"), ws[:, i % 2, :],
                                        wh[:, SLOTS[i], :, :].rearrange("p c n -> p (c n)"),
                                        ALU.subtract).then_inc(s_split, 1)

            def head_lo(n, hh):
                pool.wait_ge(s_Oh, n + 1)
                nc.gpsimd.tensor_tensor(ol[:, hh, :], of[:, hh % 2, :], oh[:, hh, :], ALU.subtract).then_inc(s_Os, 1)

            for i in range(4):
                weight_lo(i, i)
            root(1)
            root(2)
            with pool.Fori(0, B) as b:
                with pool.Fori(0, NG) as g:
                    G = b * NG + g
                    K = MATS * b + 4 * g + 4

                    def both_sines(hh):
                        sines(4 * G + hh, 0)
                        sines(4 * G + hh, 1)
                    both_sines(0)
                    both_sines(1)
                    head_lo(4 * G, 0)
                    weight_lo(K, 0)
                    both_sines(2)
                    head_lo(4 * G + 1, 1)
                    both_sines(3)
                    head_lo(4 * G + 2, 2)
                    weight_lo(K + 1, 1)
                    weight_lo(K + 2, 2)
                    head_lo(4 * G + 3, 3)
                    weight_lo(K + 3, 3)
                K = MATS * b + 4 * NG + 4
                root(4 * b + 3)
                weight_lo(K, 0)
                weight_lo(K + 1, 1)
                weight_lo(K + 2, 2)
                root(4 * b + 4)
                weight_lo(K + 3, 3)
                weight_lo(K + 4, 0)
                root(4 * b + 5)
                weight_lo(K + 5, 1)
                weight_lo(K + 6, 2)
                root(4 * b + 6)
                weight_lo(K + 7, 3)

        @block.scalar
        def _(act):
            A = nc.scalar.activation
            act.wait_ge(s_const, 128)
            A(gam[:, 2:3], vec[:, COL["gamma"]:COL["gamma"] + 1], ACT.Tanh, scale=0.5).then_inc(s_tanh, 1)
            act.sem_inc(s_OT, 1)
            act.sem_inc(s_gel, 4)
            act.sem_inc(s_out, 16)

            def col(name, i):
                return vec[:, COL[name] + i:COL[name] + i + 1]

            def weight_hi(K, i):
                act.wait_ge(s_ws[i % 2], 16 * K_half(K, i) + 16)
                nc.scalar.copy(wh[:, SLOTS[i], :, :].rearrange("p c n -> p (c n)"), ws[:, i % 2, :]).then_inc(s_wh, 1)

            def K_half(K, i):
                return K + i // 2

            def swapped(G, hh, a):
                n = 4 * G + hh
                bank = PJ + 2 * (hh % 2) + a
                bias = vec[:, bass.ds(COL["bq"] + 16 * a + n_head(hh), 1)]
                act.wait_ge(s_QK, 8 * G + 8 + 2 * hh + a + 1)
                act.wait_ge(s_rope, 2 * n + 1 + a)
                A(sh[0:64, a, :], ps[64:128, bank, :], ACT.Identity, bias=bias[64:128, :])
                A(sh[64:128, a, :], ps[0:64, bank, :], ACT.Identity, bias=bias[0:64, :]).then_inc(s_sh, 1)

            def exps(n):
                for t in range(TC):
                    act.wait_ge(s_nm, 4 * n + max(t, 1) + 1)
                    A(Pr[:, t, 0:(t + 1) * P], s_tile(t), ACT.Exp, bias=nmax[:, t:t + 1],
                      accum_out=rsum[:, t:t + 1]).then_inc(s_P, 1)

            def s_tile(t):
                return [ps[:, SA, 0:P], ps[:, SA, P:3 * P], ps[:, SB, 0:3 * P], ps[:, SC, 0:4 * P]][t]

            def pt_out(n):
                act.wait_ge(s_T, 3 * n + 1)
                nc.scalar.copy(PT[:, 0, :], ps[:, SA, :]).then_inc(s_PT, 1)
                act.wait_ge(s_T, 3 * n + 2)
                nc.scalar.copy(PT[:, 1, P:T], ps[:, SB, 0:3 * P])
                nc.scalar.copy(PT[:, 3, 3 * P:T], ps[:, SB, 3 * P:T]).then_inc(s_PT, 1)
                act.wait_ge(s_T, 3 * n + 3)
                nc.scalar.copy(PT[:, 2, 2 * P:T], ps[:, SC, 0:2 * P]).then_inc(s_PT, 1)

            def ot_out(n, g, hh):
                act.wait_ge(s_Os, n + 1)
                act.wait_ge(s_PV, n + 1)
                A(of[:, hh % 2, :], ps[:, PV, :], ACT.Identity,
                  bias=vec[:, bass.ds(COL["bv"] + 4 * g + hh, 1)]).then_inc(s_OT, 1)
                act.drain()
                nc.scalar.copy(oh[:, hh, :], of[:, hh % 2, :]).then_inc(s_Oh, 1)

            def normed(b, which, lnw, lnb):
                for c in range(C):
                    if c >= 2:
                        act.wait_ge(s_xs, 8 * b + 4 * which + c - 1)
                    act.wait_ge(s_nT, 8 * b + 4 * which + c + 1)
                    A(xf[:, c % 2, :], ps[:, PJ + c, :], ACT.Identity, bias=col(lnb, c),
                      scale=col(lnw, c)).then_inc(s_nTe, 1)

            def half_tanh(k):
                act.wait_ge(s_xin, 32 * k + 32)
                for t in range(TC):
                    A(tx[:, t, :], sx[:, t, :], ACT.Tanh, scale=0.5).then_inc(s_xth, 1)

            for i in range(4):
                weight_hi(0, i)
            half_tanh(0)
            normed(0, 0, "ln1w", "ln1b")
            with act.Fori(0, B) as b:
                with act.Fori(0, NG) as g:
                    G = b * NG + g

                    def n_head(hh):
                        return 4 * g + hh
                    act.wait_ge(s_out, 16 * b + 16)
                    K2 = MATS // 2 * b + 2 * g + 2
                    for hh in range(2):
                        swapped(G, hh, 0)
                        swapped(G, hh, 1)
                    for hh in range(GH):
                        n = 4 * G + hh
                        exps(n)
                        if hh == 0:
                            for t in range(TC):
                                act.wait_ge(s_V, 4 * G + 4 + t + 1)
                                nc.scalar.copy(Vg[:, t, :], ps[:, PJ + t, :]).then_inc(s_Ve, 1)
                            weight_hi(K2, 0)
                        if 1 <= hh < 3:
                            swapped(G, hh + 1, 0)
                            swapped(G, hh + 1, 1)
                        pt_out(n)
                        ot_out(n, g, hh)
                        if hh == 2:
                            weight_hi(K2, 1)
                            weight_hi(K2, 2)
                    act.wait_ge(s_O, 4 * G + 8)
                    weight_hi(K2, 3)
                normed(b, 1, "ln2w", "ln2b")
                for i in range(2):
                    act.wait_ge(s_lge, 2 * b + i + 1)
                    A(lg[:, 2 + 2 * i, :, :], lg[:, 1 + 2 * i, :, :], ACT.Exp).then_inc(s_lgx, 1)
                half_tanh(b + 1)
                act.wait_ge(s_cT, b + 1)
                nc.scalar.copy(combT[:, :], ps[0:E, SB, :]).then_inc(s_cTe, 1)
                K2 = MATS // 2 * b + 2 * NG + 2
                for e in range(E):
                    for i in range(C):
                        act.wait_ge(s_hs, 16 * b + 4 * e + i + 3)
                        act.wait_ge(s_h1, 16 * b + 4 * e + i + 5)
                        A(of[:, i % 2, :], ps[:, PJ + i, :], ACT.Gelu,
                          bias=col("be1", 4 * e + i)).then_inc(s_gel, 1)
                    if e == E - 1:
                        normed(b + 1, 0, "ln1w", "ln1b")
                    weight_hi(K2 + 2 * (e // 2), 2 * (e % 2))
                    act.wait_ge(s_y, 20 * b + 4 * e + 12)
                    weight_hi(K2 + 2 * (e // 2), 2 * (e % 2) + 1)
                act.wait_ge(s_fin, b + 1)
                act.dma_start(out[b], tx[:, :, :]).then_inc(s_out, 16)
            act.wait_ge(s_out, 16 * B + 16)

        @block.vector
        def _(dve):
            v = nc.vector
            dve.wait_ge(s_const, 128)
            dve.wait_ge(s_tanh, 1)
            v.tensor_scalar(gam[:, 0:1], gam[:, 2:3], 1.0, 0.125, ALU.add, ALU.mult)
            v.tensor_scalar(gam[:, 1:2], gam[:, 2:3], -0.5, 1.5, ALU.mult, ALU.add)
            dve.sem_inc(s_rope, 2)
            dve.sem_inc(s_Oe, 4)
            dve.sem_inc(s_ye, 4)
            dve.sem_inc(s_hs, 4)

            v.tensor_copy(causal[:, :], xf[:, 0, 0:P])
            v.tensor_copy(identr[:, :], ident[:, :]).then_inc(s_pre, 1)
            v.tensor_copy(wgh[:, :, :], wg[:, :, :])
            v.drain()
            v.tensor_tensor(wgl[:, :, :], wg[:, :, :], wgh[:, :, :], ALU.subtract)

            def split_normed(k, which):
                for c in range(C):
                    dve.wait_ge(s_nTe, 8 * k + 4 * which + c + 1)
                    v.tensor_copy(xh[:, c, :], xf[:, c % 2, :])
                    v.drain()
                    v.tensor_tensor(xl[:, c, :], xf[:, c % 2, :], xh[:, c, :], ALU.subtract).then_inc(s_xs, 1)

            def split_hidden(b, e):
                for i in range(C):
                    dve.wait_ge(s_gel, 16 * b + 4 * e + i + 5)
                    v.tensor_copy(oh[:, i, :], of[:, i % 2, :])
                    v.drain()
                    v.tensor_tensor(ol[:, i, :], of[:, i % 2, :], oh[:, i, :], ALU.subtract).then_inc(s_hs, 1)

            def layer_norm(k, src, dst):
                v.drain()
                for t in range(TC):
                    v.bn_stats(st[:, t, :], src[:, t, :])
                v.drain()
                for t in range(TC):
                    v.bn_aggr(mv[:, t, :], st[:, t, :])
                v.drain()
                v.tensor_scalar(var[:, :], mv[:, :, 1], EPS, None, ALU.add).then_inc(s_var, 1)
                dve.wait_ge(s_rstd, k)
                for t in range(TC):
                    ins = v.tensor_scalar(dst[:, t, :], src[:, t, :], mv[:, t, 0:1], rstd[:, t:t + 1],
                                          ALU.subtract, ALU.mult)
                return ins

            def s_tile(t):
                return [ps[:, SA, 0:P], ps[:, SA, P:3 * P], ps[:, SB, 0:3 * P], ps[:, SC, 0:4 * P]][t]

            def rotate(G, g, hh, a):
                n = 4 * G + hh
                bank = PJ + 2 * (hh % 2) + a
                dve.wait_ge(s_sh, 2 * n + a + 1)
                v.scalar_tensor_tensor(rc[:, a, :], ps[:, bank, :], vec[:, bass.ds(COL["bq"] + 16 * a + 4 * g + hh, 1)],
                                       rope[:, 2 * a, :], ALU.add, ALU.mult)
                v.drain()
                dve.wait_ge(s_rs, 2 * n + a + 1)
                v.tensor_tensor(qk[:, hh % 2, a, :], rc[:, a, :], sh[:, a, :], ALU.add).then_inc(s_rope, 1)

            def maxima(n):
                for t in range(TC):
                    if t != 1:
                        dve.wait_ge(s_S, 4 * n + max(t, 1) + 1)
                    v.tensor_reduce(nmax[:, t:t + 1], s_tile(t), AX.X, ALU.max, negate=True).then_inc(s_nm, 1)

            def normalise(n):
                for t0 in (0, 2):
                    dve.wait_ge(s_P, 4 * n + t0 + 2)
                    v.reciprocal(rinv[:, t0:t0 + 2], rsum[:, t0:t0 + 2])
                    v.drain()
                    for t in (t0, t0 + 1):
                        ins = v.tensor_scalar(Pr[:, t, 0:(t + 1) * P], Pr[:, t, 0:(t + 1) * P], rinv[:, t:t + 1],
                                              None, ALU.mult)
                ins.then_inc(s_Pn, 1)

            def threshold(k):
                v.drain()
                v.tensor_copy(thr[:, :], m8[:, :, KTH]).then_inc(s_tkdone, 1)

            def adjacency(k):
                for t in range(TC):
                    dve.wait_ge(s_xth, 4 * k + t + 1)
                    v.tensor_scalar(tx[:, t, :], tx[:, t, :], 1.0, None, ALU.add)
                v.drain()
                for t in range(TC):
                    v.scalar_tensor_tensor(sx[:, t, :], sx[:, t, :], thr[:, t:t + 1], tx[:, t, :], ALU.is_ge,
                                           ALU.mult).then_inc(s_xA, 1)
                v.drain()

            def symmetric(k):
                for t in range(TC):
                    dve.wait_ge(s_xAT, 4 * k + t + 1)
                    v.tensor_tensor(tx[:, t, :], ps[:, PJ + t, :], sx[:, t, :], ALU.add).then_inc(s_xATe, 1)
                v.drain()
                for t in range(TC):
                    v.tensor_scalar(tx[:, t, :], tx[:, t, :], gam[:, 0:1], None, ALU.mult)
                v.drain()
                for t in range(TC):
                    v.scalar_tensor_tensor(x2[:, t, :], x1[:, t, :], gam[:, 1:2], tx[:, t, :], ALU.mult, ALU.add)

            threshold(0)
            adjacency(0)
            symmetric(0)
            layer_norm(1, x2, x2)
            layer_norm(2, x2, xn).then_inc(s_xn, 1)
            split_normed(0, 0)
            for t in range(TC):
                v.tensor_tensor(h[:, t, :], x2[:, t, :], bo[:, :], ALU.add)
            with dve.Fori(0, B) as b:
                with dve.Fori(0, NG) as g:
                    G = b * NG + g
                    dve.wait_ge(s_tkin, 16 * b + 16)
                    for hh in range(2):
                        rotate(G, g, hh, 0)
                        rotate(G, g, hh, 1)
                    for hh in range(GH):
                        n = 4 * G + hh
                        maxima(n)
                        take_largest(nc, m8, tk, [hh], 2)
                        normalise(n)
                        if 1 <= hh < 3:
                            rotate(G, g, hh + 1, 0)
                            rotate(G, g, hh + 1, 1)
                        take_largest(nc, m8, tk, [hh], RPG - 2)
                    for t in range(TC):
                        dve.wait_ge(s_O, 4 * G + t + 5)
                        v.tensor_tensor(h[:, t, :], ps[:, PJ + t, :], h[:, t, :], ALU.add).then_inc(s_Oe, 1)
                layer_norm(4 * b + 3, h, xn).then_inc(s_xn, 1)
                split_normed(b, 1)
                for t in range(TC):
                    v.tensor_tensor(h[:, t, :], x2[:, t, :], h[:, t, :], ALU.add)
                threshold(b + 1)

                def over(x):
                    return x.rearrange("p (t o) -> p t o", o=1).to_broadcast([P, TC, E])
                dve.wait_ge(s_lg, b + 1)
                v.tensor_copy(lg[:, 0, :, :], ps[:, SA, 0:TC * E].rearrange("p (t e) -> p t e", e=E))
                v.drain()
                v.tensor_reduce(r1[:, 0, :], lg[:, 0, :, :], AX.X, ALU.max)
                v.drain()
                v.tensor_tensor(lg[:, 1, :, :], lg[:, 0, :, :], over(r1[:, 0, :]), ALU.subtract).then_inc(s_lge, 1)
                dve.wait_ge(s_lgx, 2 * b + 1)
                v.tensor_reduce(r1[:, 1, :], lg[:, 2, :, :], AX.X, ALU.add)
                v.drain()
                v.reciprocal(r1[:, 2, :], r1[:, 1, :])
                v.drain()
                v.tensor_tensor(lg[:, 0, :, :], lg[:, 2, :, :], over(r1[:, 2, :]), ALU.mult)
                v.drain()
                v.tensor_reduce(r1[:, 3, :], lg[:, 0, :, :], AX.X, ALU.max)
                for j in range(E):
                    pj = lg[:, 0, :, j:j + 1].to_broadcast([P, TC, E])
                    v.tensor_tensor(cmp_[:, 0, :, :, j], pj, lg[:, 0, :, :], ALU.is_gt)
                    v.tensor_tensor(cmp_[:, 1, :, :, j], pj, lg[:, 0, :, :], ALU.is_equal)
                v.drain()
                v.tensor_tensor(cmp_[:, 2, :, :, :], cmp_[:, 1, :, :, :], before[:, :, :, :], ALU.mult)
                v.tensor_tensor(lg[:, 3, :, :], lg[:, 0, :, :], over(r1[:, 3, :]), ALU.subtract).then_inc(s_lge, 1)
                v.drain()
                v.tensor_tensor(cmp_[:, 1, :, :, :], cmp_[:, 0, :, :, :], cmp_[:, 2, :, :, :], ALU.add)
                v.drain()
                v.tensor_reduce(lg[:, 5, :, :], cmp_[:, 1, :, :, :], AX.X, ALU.add)
                v.drain()
                dve.wait_ge(s_lgx, 2 * b + 2)
                v.scalar_tensor_tensor(lg[:, 1, :, :], lg[:, 5, :, :], 2.0, lg[:, 4, :, :], ALU.is_lt, ALU.mult)
                v.drain()
                v.tensor_reduce(r1[:, 4, :], lg[:, 1, :, :], AX.X, ALU.add)
                v.drain()
                v.reciprocal(r1[:, 5, :], r1[:, 4, :])
                v.drain()
                v.tensor_tensor(lg[:, 5, :, :], lg[:, 1, :, :], over(r1[:, 5, :]), ALU.mult).then_inc(s_comb, 1)

                def add_expert(e):
                    for t in range(TC):
                        v.drain()
                        dve.wait_ge(s_y, 20 * b + 4 * e + t + 9)
                        v.scalar_tensor_tensor(h[:, t, :], ps[:, SA + t, :], lg[:, 5, t, e:e + 1], h[:, t, :],
                                               ALU.mult, ALU.add).then_inc(s_ye, 1)

                adjacency(b + 1)
                for t in range(TC):
                    dve.wait_ge(s_y, 20 * b + t + 5)
                    v.tensor_tensor(h[:, t, :], ps[:, SA + t, :], h[:, t, :], ALU.add).then_inc(s_ye, 1)
                split_hidden(b, 0)
                symmetric(b + 1)
                add_expert(0)
                split_hidden(b, 1)
                layer_norm(4 * b + 4, x2, x2)
                add_expert(1)
                split_hidden(b, 2)
                layer_norm(4 * b + 5, x2, xn).then_inc(s_xn, 1)
                add_expert(2)
                split_hidden(b, 3)
                split_normed(b + 1, 0)
                add_expert(3)
                layer_norm(4 * b + 6, h, tx).then_inc(s_fin, 1)
                v.drain()
                for t in range(TC):
                    v.tensor_tensor(h[:, t, :], x2[:, t, :], bo[:, :], ALU.add)

        @block.tensor
        def _(pe):
            mm = nc.tensor.matmul
            tr = nc.tensor.transpose
            pe.wait_ge(s_const, 128)
            pe.wait_ge(s_pre, 1)
            pe.sem_inc(s_QK, 8)
            pe.sem_inc(s_V, 4)
            pe.sem_inc(s_O, 4)
            pe.sem_inc(s_h1, 4)
            pe.sem_inc(s_y, 4)

            def product(dst, terms, first=True, last=True):
                for j, (ah, al, bh, bl) in enumerate(terms):
                    start, stop = first and j == 0, last and j == len(terms) - 1
                    mm(dst, ah, bh, start=start, stop=False, skip_group_check=True)
                    mm(dst, ah, bl, start=False, stop=False, skip_group_check=True)
                    ins = mm(dst, al, bh, start=False, stop=stop, skip_group_check=True)
                return ins

            def ready(K):
                pe.wait_ge(s_split, K + 3)

            def transposed(b, which):
                pe.wait_ge(s_xn, 2 * b + which + 1)
                for c in range(C):
                    for t in range(TC):
                        ins = tr(ps[:, PJ + c, t * P:(t + 1) * P], xn[:, t, c * P:(c + 1) * P], ident[:, :])
                    ins.then_inc(s_nT, 1)

            def project_qk(G, K, hh):
                for a in range(2):
                    bank = PJ + 2 * (hh % 2) + a
                    if hh < 2:
                        pe.wait_ge(s_Oe, 4 * G + 2 * hh + a + 1)
                    else:
                        pe.wait_ge(s_Ve, 4 * G + 2 * (hh - 2) + a + 1)
                    if hh == 0:
                        ready(K + 1 + a)
                    cols = slice(hh * P, (hh + 1) * P)
                    product(ps[:, bank, :], [(wh[:, a, k, cols], wl[:, a, k, cols], xh[:, k, :], xl[:, k, :])
                                             for k in range(C)]).then_inc(s_QK, 1)

            def scores(n, hh):
                pe.wait_ge(s_rope, 2 * n + 4)
                q, k = qk[:, hh % 2, 0, :], qk[:, hh % 2, 1, :]
                for t, dst in enumerate([ps[:, SA, 0:P], ps[:, SA, P:3 * P], ps[:, SB, 0:3 * P], ps[:, SC, 0:4 * P]]):
                    mm(dst, q[:, t * P:(t + 1) * P], k[:, 0:(t + 1) * P], start=True, stop=False,
                       skip_group_check=True)
                    mm(dst[:, t * P:(t + 1) * P], identr[:, :], causal[:, :], start=False, stop=True,
                       skip_group_check=True).then_inc(s_S, 1)

            def values(G):
                for t in range(TC):
                    pe.wait_ge(s_rope, 8 * G + t + 3)
                    rows = slice(t * P, (t + 1) * P)
                    product(ps[:, PJ + t, :], [(xh[:, k, rows], xl[:, k, rows], wh[:, 2, k, :], wl[:, 2, k, :])
                                               for k in range(C)]).then_inc(s_V, 1)

            def transpose_probs(n):
                pe.wait_ge(s_Pn, n + 1)
                for t in range(TC):
                    ins = tr(ps[:, SA, t * P:(t + 1) * P], Pr[:, t, 0:P], ident[:, :])
                ins.then_inc(s_T, 1)
                for t in range(1, TC):
                    tr(ps[:, SB, (t - 1) * P:t * P], Pr[:, t, P:2 * P], ident[:, :])
                tr(ps[:, SB, 3 * P:T], Pr[:, 3, 3 * P:T], ident[:, :]).then_inc(s_T, 1)
                for t in range(2, TC):
                    ins = tr(ps[:, SC, (t - 2) * P:(t - 1) * P], Pr[:, t, 2 * P:3 * P], ident[:, :])
                ins.then_inc(s_T, 1)

            def weigh_values(G, n, hh):
                if hh == 0:
                    pe.wait_ge(s_Ve, 4 * G + 4)
                pe.wait_ge(s_OT, n + 1)
                for i, j in enumerate((0, 1, 3, 2)):
                    pe.wait_ge(s_PT, 3 * n + (1, 2, 2, 3)[i])
                    ins = mm(ps[:, PV, j * P:T], Vg[:, j, hh * P:(hh + 1) * P], PT[:, j, j * P:T], start=(i == 0),
                             stop=(i == 3), skip_group_check=True)
                ins.then_inc(s_PV, 1)

            def project_out(G, heads):
                for t in range(TC):
                    if heads[0] == 0:
                        pe.wait_ge(s_rope, 8 * G + t + 7)
                    rows = slice(t * P, (t + 1) * P)
                    ins = product(ps[:, PJ + t, :], [(oh[:, hh, rows], ol[:, hh, rows], wh[:, 3, hh, :],
                                                      wl[:, 3, hh, :]) for hh in heads],
                                  first=heads[0] == 0, last=heads[-1] == GH - 1)
                    if heads[-1] == GH - 1:
                        ins.then_inc(s_O, 1)

            def transposed_adjacency(k):
                pe.wait_ge(s_xA, 4 * k + 4)
                for t in range(TC):
                    for m in range(TC):
                        ins = tr(ps[:, PJ + t, m * P:(m + 1) * P], sx[:, m, t * P:(t + 1) * P], ident[:, :])
                    ins.then_inc(s_xAT, 1)

            transposed_adjacency(0)
            transposed(0, 0)
            with pe.Fori(0, B) as b:
                with pe.Fori(0, NG) as g:
                    G = b * NG + g
                    K = MATS * b + 4 * g
                    pe.wait_ge(s_xs, 8 * b + 4)
                    project_qk(G, K, 0)
                    project_qk(G, K, 1)
                    for hh in range(GH):
                        n = 4 * G + hh
                        scores(n, hh)
                        if hh == 0:
                            values(G)
                        elif hh < 3:
                            project_qk(G, K, hh + 1)
                        else:
                            ready(K + 3)
                            pe.wait_ge(s_Os, n + 2)
                            project_out(G, range(3))
                        transpose_probs(n)
                        weigh_values(G, n, hh)
                    pe.wait_ge(s_Os, 4 * G + 6)
                    project_out(G, [3])
                transposed(b, 1)
                pe.wait_ge(s_xs, 8 * b + 8)
                for t in range(TC):
                    rows = slice(t * P, (t + 1) * P)
                    ins = product(ps[:, SA, t * E:(t + 1) * E], [(xh[:, k, rows], xl[:, k, rows], wgh[:, k, :],
                                                                  wgl[:, k, :]) for k in range(C)])
                ins.then_inc(s_lg, 1)

                KE = MATS * b + 4 * NG

                def expert_in(e):
                    ready(KE + 2 * e)
                    slot = (2, 1)[e % 2]
                    for i in range(C):
                        pe.wait_ge(s_gel, 16 * b + 4 * e + i + 1)
                        if e == 1:
                            pe.wait_ge(s_xATe, 4 * b + i + 5)
                        cols = slice(i * P, (i + 1) * P)
                        product(ps[:, PJ + i, :], [(wh[:, slot, k, cols], wl[:, slot, k, cols], xh[:, k, :],
                                                    xl[:, k, :]) for k in range(C)]).then_inc(s_h1, 1)

                def expert_out(e):
                    ready(KE + 2 * e + 1)
                    slot = (0, 3)[e % 2]
                    pe.wait_ge(s_hs, 16 * b + 4 * e + 8)
                    for t in range(TC):
                        pe.wait_ge(s_ye, 20 * b + 4 * e + t + 5)
                        rows = slice(t * P, (t + 1) * P)
                        product(ps[:, SA + t, :], [(oh[:, i, rows], ol[:, i, rows], wh[:, slot, i, :],
                                                    wl[:, slot, i, :]) for i in range(C)]).then_inc(s_y, 1)

                expert_in(0)
                pe.wait_ge(s_comb, b + 1)
                for t in range(TC):
                    ins = tr(ps[0:E, SB, t * P:(t + 1) * P], lg[:, 5, t, :], ident[:, :])
                ins.then_inc(s_cT, 1)
                pe.wait_ge(s_cTe, b + 1)
                for t in range(TC):
                    mm(ps[:, SA + t, :], combT[:, t * P:(t + 1) * P], be2[:, :], start=True, stop=True).then_inc(s_y, 1)
                pe.wait_ge(s_gel, 16 * b + 8)
                transposed_adjacency(b + 1)
                expert_out(0)
                for e in range(1, E):
                    expert_in(e)
                    if e == E - 1:
                        pe.wait_ge(s_gel, 16 * b + 20)
                        transposed(b + 1, 0)
                    expert_out(e)


def decoder(nc, dram, out):
    x1_d = nc.dram_tensor("x1_scratch", (B, P, TC, D), F32, kind="Internal").ap()
    sim_d = nc.dram_tensor("sim_scratch", (B, P, TC, T), F32, kind="Internal").ap()
    with nc.sbuf_tensor("m8", [P, TC, 8], F32) as m8:
        block_a(nc, dram, x1_d, sim_d, m8)
        block_c(nc, dram, x1_d, sim_d, m8, out)


def rope_tables():
    f = np.float32
    inv = f(1.0) / np.power(f(10000.0), np.arange(0, P, 2, dtype=f) / f(P)).astype(f)
    ang = (np.arange(T, dtype=f)[:, None] * inv[None, :]).astype(f)
    ang = np.concatenate([ang, ang], 1).T
    cos, sin = np.cos(ang).astype(f), np.sin(ang).astype(f)
    sin[:P // 2] *= -1
    s = f(P ** -0.5)
    return np.ascontiguousarray(np.stack([cos * s, sin * s, cos, sin], 1))


def kernel(**inputs):
    from concourse import bacc
    from concourse.bass_utils import run_bass_kernel_spmd

    a = {k: np.asarray(v) for k, v in inputs.items()}

    def rows(w):
        return w.reshape(-1, P, w.shape[-1]).transpose(1, 0, 2)

    def feat(w):
        return w.reshape(-1, P).T

    def tokens(x):
        return x.reshape(B, TC, P, -1).transpose(0, 2, 1, 3)

    f = "L0_ffn_"
    r = "L0_attn_"
    vec = np.concatenate(
        [feat(a[r + "time_mix_" + n]) for n in ("key", "value", "receptance")]
        + [feat(a[r + "time_decay"]), feat(a[r + "time_first"])]
        + [feat(a[f + n]) for n in ("bq", "bk", "bv", "ln1_w", "ln1_b", "ln2_w", "ln2_b", "be1")]
        + [np.broadcast_to(a["L0_xattn_gamma_raw"].reshape(1, 1), (P, 1))], axis=1)
    xT = a["x"].reshape(B, T, C, P).transpose(0, 3, 2, 1)
    groups = (C, P, NG, GH * P)
    by_group = np.stack([a[f + n].reshape(groups).transpose(2, 1, 0, 3) for n in ("wv", "wq", "wk")]
                        + [a[f + "wo"].reshape(NG, GH, P, D).transpose(0, 2, 1, 3)], 1)
    by_expert = np.stack([w.reshape(E, C, P, D).transpose(0, 2, 1, 3) for w in (a[f + "we1"], a[f + "we2"])], 1)
    by_expert = by_expert.reshape(E // 2, 4, P, C, D)
    before = np.broadcast_to((np.arange(E)[None, :] < np.arange(E)[:, None]).astype(np.float32), (P, TC, E, E))
    q = np.arange(P)
    arrays = {
        "vec": vec,
        "wqkT": np.stack([a["L0_xattn_Wq"].T, a["L0_xattn_Wk"].T], 1),
        "W": np.stack([rows(a[r + n]) for n in ("Wk", "Wv", "Wr", "Wo")]),
        "x": tokens(a["x"]),
        "xT": np.pad(xT, ((0, 0), (0, 0), (0, 0), (1, 0))),
        "cT": a["ctx_512"].transpose(0, 2, 1),
        "ident": np.eye(P, dtype=np.float32),
        "rope": rope_tables(),
        "causal": np.where(q[None, :] > q[:, None], np.float32(NEG), np.float32(0)),
        "before": before,
        "bo": np.broadcast_to(a[f + "bo"], (P, D)),
        "wg": rows(a[f + "w_gate"]),
        "be2": a[f + "be2"],
        "wset": np.concatenate([by_group, by_expert]).reshape(SETS, 4, P, C * D),
    }
    arrays = {k: np.ascontiguousarray(w) for k, w in arrays.items()}
    nc = bacc.Bacc("TRN2", target_bir_lowering=False, num_devices=1)
    dram = {k: nc.dram_tensor("in_" + k, w.shape, mybir.dt.from_np(w.dtype), kind="ExternalInput").ap()
            for k, w in arrays.items()}
    out = nc.dram_tensor("out_x", (B, P, TC, D), F32, kind="ExternalOutput").ap()
    decoder(nc, dram, out)
    res = run_bass_kernel_spmd(nc, [{"in_" + k: w for k, w in arrays.items()}], core_ids=[0])
    y = res.results[0]["out_x"]
    return y.transpose(0, 2, 1, 3).reshape(B, T, D)
```

```python
from contextlib import ExitStack

import numpy as np

import concourse.bass as bass
from concourse import mybir

F32 = mybir.dt.float32
F32R = mybir.dt.float32r
ALU = mybir.AluOpType
ACT = mybir.ActivationFunctionType
AX = mybir.AxisListType

P = 128
B, T, D = 4, 512, 512
C = D // P
TC = T // P
HEADS = 16
GH = 4
NG = HEADS // GH
E = 4
DM = 128
XHEADS = 4
TOPK = int(T * 0.3)
ROUNDS = -(-TOPK // 8)
RPG = ROUNDS // NG
KTH = (TOPK - 1) % 8
START, BEFORE, AFTER = 2, (2, 2, 2, 2), (4, 2, 2, 2)
assert ROUNDS == RPG * NG and START + sum(BEFORE) + sum(AFTER) == RPG * TC
EPS = 1e-5
SIM_SCALE = float(1.0 / (np.sqrt(np.float32(DM // XHEADS)) * XHEADS))
NEG = -1e30
MX0 = -1e38

SETS = NG + E // 2
MATS = 4 * SETS
SLOTS = (2, 0, 1, 3)
COL = {}
_n = 0
for _name, _w in [("mix", 12), ("decay", 4), ("first", 4), ("bq", 16), ("bk", 16), ("bv", 16),
                  ("ln1w", 4), ("ln1b", 4), ("ln2w", 4), ("ln2b", 4), ("be1", 16), ("gamma", 1)]:
    COL[_name] = _n
    _n += _w
NCOL = _n


def take_largest(nc, m8, tk, tiles, rounds):
    v = nc.vector
    for _ in range(rounds):
        for t in tiles:
            v.max(m8[:, t, :], tk[:, t, :])
        v.drain()
        for t in tiles:
            v.match_replace(tk[:, t, :], m8[:, t, :], tk[:, t, :], NEG)
        v.drain()


def block_a(nc, dram, x1_d, sim_d, m8):
    with ExitStack() as ctx:
        def sb(name, shape):
            return ctx.enter_context(nc.sbuf_tensor(name, shape, F32))

        def sem(name):
            return ctx.enter_context(nc.semaphore(name))

        W = sb("W", [P, 4, C, D])
        vec = sb("vecA", [P, NCOL])
        omm = sb("omm", [P, 12])
        td = sb("td", [P, C])
        wqk = sb("wqk", [P, 2, DM])
        xT = sb("xT", [P, C, T + 1])
        xr = sb("xr", [P, TC, D])
        cT = sb("cT", [P, T])
        tmp = sb("tmp", [P, 2, 2, T])
        mk = sb("mk", [P, 3, C, T])
        qk = sb("qkA", [P, 2, T])
        sim = sb("simA", [P, TC, T])
        Mx = sb("Mx", [P, T + 1])
        dg = sb("dg", [P, 2, 2, T])
        rr = sb("rr", [P, 2, 2, T])
        ee = sb("ee", [P, 2, 4, T])
        Dn = sb("Dn", [P, 2, T + 1])
        Nm = sb("Nm", [P, 2, T + 1])
        vs = sb("vs", [P, C, T])
        th = sb("th", [P, C, T])
        ev = sb("ev", [P, 2, T])
        p2 = sb("p2", [P, 2, T])
        rec = sb("rec", [P, 2, T])
        num2 = sb("num2", [P, 2, T])
        rw = sb("rw", [P, C, T])
        z = sb("z", [P, TC, D])
        st = sb("stA", [P, TC, 6])
        mv = sb("mvA", [P, TC, 2])
        var = sb("varA", [P, TC])
        mhalf = sb("mhalfA", [P, TC])
        rstd = sb("rstdA", [P, TC])
        x1 = z
        tk = sb("tkA", [P, TC, T])
        ps = ctx.enter_context(nc.psum_tensor("psA", [P, 8, 512], F32))
        E1, E2S, E2, E1S = 0, 1, 2, 3
        Y = 6

        s_const = sem("a_const")
        s_W = sem("a_W")
        s_xT = sem("a_xT")
        s_xr = sem("a_xr")
        s_cT = sem("a_cT")
        s_pre = sem("a_pre")
        s_half = sem("a_half")
        s_sh = sem("a_sh")
        s_mix = sem("a_mix")
        s_proj = sem("a_proj")
        s_dg = sem("a_dg")
        s_free = sem("a_free")
        s_vt = sem("a_vt")
        s_e = sem("a_e")
        s_ev = sem("a_ev")
        s_scan = sem("a_scan")
        s_pq = sem("a_pq")
        s_rw = sem("a_rw")
        s_sps = sem("a_sps")
        s_sev = sem("a_sev")
        s_y = sem("a_y")
        s_z = sem("a_z")
        s_var = sem("a_var")
        s_rstd = sem("a_rstd")
        s_x1 = sem("a_x1")
        s_x1o = sem("a_x1o")
        s_simo = sem("a_simo")

        block = ctx.enter_context(nc.Block())

        @block.sync
        def _(sp):
            sp.dma_start(xT[:, :, :], dram["xT"][0]).then_inc(s_xT, 16)
            sp.dma_start(vec[:, :], dram["vec"]).then_inc(s_const, 16)
            sp.dma_start(wqk[:, :, :], dram["wqkT"]).then_inc(s_const, 16)
            sp.dma_start(cT[:, :], dram["cT"][0]).then_inc(s_cT, 16)
            for i in range(4):
                sp.dma_start(W[:, i, :, :], dram["W"][i]).then_inc(s_W, 16)
            sp.dma_start(xr[:, :, :], dram["x"][0]).then_inc(s_xr, 16)
            sp.sem_inc(s_x1o, 16)
            sp.sem_inc(s_simo, 16)
            sp.wait_ge(s_sh, 12)
            sp.dma_start(xT[:, :, :], dram["xT"][1]).then_inc(s_xT, 16)

            def store_sim(b):
                sp.wait_ge(s_sev, 6 * b + 12)
                sp.dma_start(sim_d[b], sim[:, :, :]).then_inc(s_simo, 16)

            def store_x1(b):
                sp.wait_ge(s_x1, b + 1)
                sp.dma_start(x1_d[b], x1[:, :, :]).then_inc(s_x1o, 16)

            with sp.Fori(0, B - 1) as b:
                sp.wait_ge(s_sps, 6 * b + 8)
                sp.dma_start(cT[:, :], dram["cT"][b + 1]).then_inc(s_cT, 16)
                sp.wait_ge(s_sh, 12 * b + 24)
                sp.dma_start(xT[:, :, :], dram["xT"][(b + 2) % B]).then_inc(s_xT, 16)
                store_sim(b)
                sp.wait_ge(s_z, 4 * b + 4)
                sp.dma_start(xr[:, :, :], dram["x"][b + 1]).then_inc(s_xr, 16)
                store_x1(b)
            store_sim(B - 1)
            store_x1(B - 1)
            sp.wait_ge(s_simo, 16 * B + 16)
            sp.wait_ge(s_x1o, 16 * B + 16)
            sp.wait_ge(s_xT, 16 * B + 16)

        @block.gpsimd
        def _(pool):
            nc.gpsimd.memset(mhalf[:, :], -0.5).then_inc(s_half, 1)
            pool.wait_ge(s_half, 1)

            def ev_products(b, c):
                i = c % 2
                pool.wait_ge(s_vt, 4 * b + c + 3)
                pool.wait_ge(s_e, 4 * b + c + 1)
                nc.gpsimd.tensor_tensor(ev[:, i, :], ee[:, i, E2S, :], vs[:, c, :], ALU.mult).then_inc(s_ev, 1)
                nc.gpsimd.tensor_tensor(p2[:, i, :], ee[:, i, E2, :], vs[:, c, :], ALU.mult).then_inc(s_ev, 1)

            def sum_products(b, c):
                i = c % 2
                pool.wait_ge(s_scan, 4 * b + c + 1)
                nc.gpsimd.tensor_tensor(ee[:, i, E2S, :], ee[:, i, E1, :], Dn[:, i, 0:T], ALU.mult).then_inc(s_pq, 1)
                nc.gpsimd.tensor_tensor(ev[:, i, :], ee[:, i, E1, :], Nm[:, i, 0:T], ALU.mult).then_inc(s_pq, 1)

            def mixes(bm, c):
                for m in range(3):
                    j = 3 * c + m
                    pool.wait_ge(s_sh, 12 * bm + j + 1)
                    nc.gpsimd.tensor_tensor(mk[:, m, c, :], tmp[:, j % 2, 0, :], tmp[:, j % 2, 1, :],
                                            ALU.add).then_inc(s_mix, 1)

            def root(b):
                pool.wait_ge(s_var, b + 2)
                nc.gpsimd.tensor_tensor(rstd[:, :], var[:, :], mhalf[:, :], ALU.pow).then_inc(s_rstd, 1)

            pool.sem_inc(s_mix, 2)
            for c in range(C):
                mixes(0, c)
            for c in range(2):
                ev_products(0, c)
                sum_products(0, c)
            with pool.Fori(0, B - 1) as b:
                pool.wait_ge(s_proj, 12 * b + 12)
                mixes(b + 1, 0)
                ev_products(b, 2)
                mixes(b + 1, 1)
                sum_products(b, 2)
                mixes(b + 1, 2)
                root(b - 1)
                mixes(b + 1, 3)
                ev_products(b, 3)
                sum_products(b, 3)
                for c in range(2):
                    ev_products(b + 1, c)
                    sum_products(b + 1, c)
            ev_products(B - 1, 2)
            sum_products(B - 1, 2)
            root(B - 2)
            ev_products(B - 1, 3)
            sum_products(B - 1, 3)
            root(B - 1)

        @block.scalar
        def _(act):
            act.wait_ge(s_const, 32)
            nc.scalar.activation(td[:, :], vec[:, COL["decay"]:COL["decay"] + C], ACT.Exp).then_inc(s_pre, 1)
            act.wait_ge(s_pre, 5)
            act.sem_inc(s_vt, 2)

            def mix_products(bm, c):
                for m in range(3):
                    j = 3 * c + m
                    act.wait_ge(s_mix, 12 * bm + j + 1)
                    nc.scalar.mul(tmp[:, j % 2, 0, :], xT[:, c, 1:T + 1],
                                  vec[:, COL["mix"] + 4 * m + c:COL["mix"] + 4 * m + c + 1])
                    nc.scalar.mul(tmp[:, j % 2, 1, :], xT[:, c, 0:T],
                                  omm[:, 4 * m + c:4 * m + c + 1]).then_inc(s_sh, 1)

            def v_and_r(b, c):
                act.wait_ge(s_free, 4 * b + c + 1)
                act.wait_ge(s_proj, 12 * b + 3 * c + 2)
                nc.scalar.copy(vs[:, c, :], ps[:, 3 * (c % 2) + 1, :])
                act.wait_ge(s_proj, 12 * b + 3 * c + 3)
                nc.scalar.activation(th[:, c, :], ps[:, 3 * (c % 2) + 2, :], ACT.Tanh, scale=0.5).then_inc(s_vt, 1)

            def exponentials(b, c):
                i = c % 2
                act.drain()
                act.wait_ge(s_free, 4 * b + c + 3)
                act.wait_ge(s_dg, 4 * b + c + 3)
                nc.scalar.activation(rr[:, 0, :, :], dg[:, i, :, :], ACT.Relu)
                nc.scalar.activation(rr[:, 1, :, :], dg[:, i, :, :], ACT.Relu, scale=-1.0)
                act.drain()
                nc.scalar.activation(ee[:, i, :, :].rearrange("p a t -> p (a t)"),
                                     rr[:, :, :, :].rearrange("p a c t -> p (a c t)"), ACT.Exp,
                                     scale=-1.0).then_inc(s_e, 1)

            def qk_out(b):
                for j in range(2):
                    act.wait_ge(s_sps, 6 * b + j + 7)
                    nc.scalar.copy(qk[:, j, :], ps[:, Y + j, :]).then_inc(s_sev, 1)

            def sim_out(b, tiles):
                for t in tiles:
                    act.wait_ge(s_sps, 6 * b + t + 9)
                    nc.scalar.mul(sim[:, t, :], ps[:, Y + t % 2, :], SIM_SCALE).then_inc(s_sev, 1)

            act.wait_ge(s_xT, 16)
            for c in range(C):
                mix_products(0, c)
            for j in range(2):
                act.wait_ge(s_sps, j + 1)
                nc.scalar.copy(qk[:, j, :], ps[:, Y + j, :]).then_inc(s_sev, 1)
            for t in range(TC):
                act.wait_ge(s_sps, t + 3)
                nc.scalar.mul(tk[:, t, :], ps[:, Y + t % 2, :], SIM_SCALE).then_inc(s_sev, 1)
            v_and_r(0, 0)
            exponentials(0, 0)
            v_and_r(0, 1)
            exponentials(0, 1)
            v_and_r(0, 2)
            with act.Fori(0, B - 1) as b:
                v_and_r(b, 3)
                act.wait_ge(s_xT, 16 * b + 32)
                mix_products(b + 1, 0)
                exponentials(b, 2)
                mix_products(b + 1, 1)
                mix_products(b + 1, 2)
                mix_products(b + 1, 3)
                exponentials(b, 3)
                qk_out(b)
                v_and_r(b + 1, 0)
                exponentials(b + 1, 0)
                act.wait_ge(s_simo, 16 * b + 16)
                sim_out(b, (0, 1))
                v_and_r(b + 1, 1)
                exponentials(b + 1, 1)
                sim_out(b, (2, 3))
                v_and_r(b + 1, 2)
            v_and_r(B - 1, 3)
            exponentials(B - 1, 2)
            qk_out(B - 1)
            exponentials(B - 1, 3)
            act.wait_ge(s_simo, 16 * B)
            sim_out(B - 1, range(TC))

        @block.vector
        def _(dve):
            v = nc.vector
            v.memset(Mx[:, 0:1], MX0).then_inc(s_pre, 1)
            v.memset(Dn[:, :, 0:1], 0.0).then_inc(s_pre, 1)
            v.memset(Nm[:, :, 0:1], 0.0).then_inc(s_pre, 1)
            dve.wait_ge(s_const, 32)
            v.tensor_scalar(omm[:, :], vec[:, 0:12], -1.0, 1.0, ALU.mult, ALU.add).then_inc(s_pre, 1)
            dve.wait_ge(s_pre, 5)
            v.tensor_scalar(td[:, :], td[:, :], -1.0, None, ALU.mult)
            dve.sem_inc(s_dg, 2)
            dve.sem_inc(s_free, 4)
            v.memset(var[:, :], 1.0).then_inc(s_var, 1)

            def exponents(b, c):
                k = ps[:, 3 * (c % 2), :]
                v.drain()
                dve.wait_ge(s_proj, 12 * b + 3 * c + 1)
                v.tensor_tensor_scan(Mx[:, 1:T + 1], td[:, c:c + 1].to_broadcast([P, T]), k, MX0, ALU.add, ALU.max)
                v.drain()
                v.scalar_tensor_tensor(dg[:, c % 2, 0, :], k, vec[:, COL["first"] + c:COL["first"] + c + 1],
                                       Mx[:, 0:T], ALU.add, ALU.subtract)
                v.scalar_tensor_tensor(dg[:, c % 2, 1, :], Mx[:, 0:T], td[:, c:c + 1], k, ALU.add,
                                       ALU.subtract).then_inc(s_dg, 1)

            def sums(b, c):
                i = c % 2
                dve.wait_ge(s_e, 4 * b + c + 1)
                v.tensor_tensor_scan(Dn[:, i, 1:T + 1], ee[:, i, E1S, :], ee[:, i, E2S, :], 0.0, ALU.mult, ALU.add)
                dve.wait_ge(s_ev, 8 * b + 2 * c + 1)
                v.tensor_tensor_scan(Nm[:, i, 1:T + 1], ee[:, i, E1S, :], ev[:, i, :], 0.0, ALU.mult,
                                     ALU.add).then_inc(s_scan, 1)

            def outputs(b, c):
                i = c % 2
                v.drain()
                dve.wait_ge(s_pq, 8 * b + 2 * c + 2)
                v.tensor_tensor(ee[:, i, E2S, :], ee[:, i, E2S, :], ee[:, i, E2, :], ALU.add)
                v.tensor_tensor(ev[:, i, :], ev[:, i, :], p2[:, i, :], ALU.add)
                v.drain()
                v.reciprocal(rec[:, min(c, 1), :], ee[:, i, E2S, :])
                v.scalar_tensor_tensor(num2[:, min(c, 1), :], th[:, c, :], 1.0, ev[:, i, :], ALU.add,
                                       ALU.mult).then_inc(s_free, 1)

            def gated(c):
                v.drain()
                v.scalar_tensor_tensor(rw[:, c, :], num2[:, min(c, 1), :], 0.5, rec[:, min(c, 1), :], ALU.mult,
                                       ALU.mult).then_inc(s_rw, 1)

            def residual(b, tiles):
                for t in tiles:
                    dve.wait_ge(s_y, 4 * b + t + 1)
                    v.tensor_tensor(z[:, t, :], ps[:, Y + t % 2, :], xr[:, t, :], ALU.add).then_inc(s_z, 1)

            def variances(b):
                v.drain()
                for t in range(TC):
                    v.bn_stats(st[:, t, :], z[:, t, :])
                v.drain()
                for t in range(TC):
                    v.bn_aggr(mv[:, t, :], st[:, t, :])
                v.drain()
                dve.wait_ge(s_rstd, b + 1)
                v.tensor_scalar(var[:, :], mv[:, :, 1], EPS, None, ALU.add).then_inc(s_var, 1)

            def normalised(b):
                dve.wait_ge(s_rstd, b + 2)
                for t in range(TC):
                    ins = v.tensor_scalar(x1[:, t, :], z[:, t, :], mv[:, t, 0:1], rstd[:, t:t + 1],
                                          ALU.subtract, ALU.mult)
                ins.then_inc(s_x1, 1)

            def search():
                take_largest(nc, m8, tk, range(TC), 1)

            dve.wait_ge(s_sev, 6)
            search()
            exponents(0, 0)
            search()
            sums(0, 0)
            exponents(0, 1)
            search()
            sums(0, 1)
            exponents(0, 2)
            outputs(0, 0)
            gated(0)
            sums(0, 2)
            exponents(0, 3)
            outputs(0, 1)
            gated(1)
            with dve.Fori(0, B - 1) as b:
                search()
                sums(b, 3)
                outputs(b, 2)
                gated(2)
                exponents(b + 1, 0)
                search()
                sums(b + 1, 0)
                exponents(b + 1, 1)
                outputs(b, 3)
                gated(3)
                search()
                sums(b + 1, 1)
                exponents(b + 1, 2)
                outputs(b + 1, 0)
                search()
                dve.wait_ge(s_xr, 16 * b + 16)
                dve.wait_ge(s_x1o, 16 * b + 16)
                residual(b, (0, 1))
                sums(b + 1, 2)
                exponents(b + 1, 3)
                residual(b, (2, 3))
                variances(b)
                search()
                normalised(b)
                gated(0)
                outputs(b + 1, 1)
                gated(1)
            search()
            sums(B - 1, 3)
            outputs(B - 1, 2)
            gated(2)
            search()
            outputs(B - 1, 3)
            gated(3)
            dve.wait_ge(s_xr, 16 * B)
            dve.wait_ge(s_x1o, 16 * B)
            residual(B - 1, range(TC))
            variances(B - 1)
            normalised(B - 1)

        @block.tensor
        def _(pe):
            mm = nc.tensor.matmul
            pe.wait_ge(s_const, 32)

            def project(b, c):
                pe.wait_ge(s_dg, 4 * b + c + 1)
                pe.wait_ge(s_vt, 4 * b + c + 1)
                if c == 0:
                    pe.wait_ge(s_mix, 12 * b + 14)
                for m in range(3):
                    for k in range(C):
                        ins = mm(ps[:, 3 * (c % 2) + m, :], W[:, m, k, c * P:(c + 1) * P], mk[:, m, k, :],
                                 start=(k == 0), stop=(k == C - 1))
                    ins.then_inc(s_proj, 1)

            def context_qk():
                for j in range(2):
                    mm(ps[:, Y + j, :], wqk[:, j, :], cT[:, :], start=True, stop=True).then_inc(s_sps, 1)

            def similarities(n, tiles):
                for t in tiles:
                    pe.wait_ge(s_sev, n + max(t, 1) + 1)
                    mm(ps[:, Y + t % 2, :], qk[:, 0, t * P:(t + 1) * P], qk[:, 1, :], start=True,
                       stop=True).then_inc(s_sps, 1)

            def project_out(b):
                pe.wait_ge(s_sev, 6 * b + 12)
                pe.wait_ge(s_rw, 4 * b + 4)
                for t in range(TC):
                    if t >= 2:
                        pe.wait_ge(s_z, 4 * b + t - 1)
                    for c in range(C):
                        ins = mm(ps[:, Y + t % 2, :], rw[:, c, t * P:(t + 1) * P], W[:, 3, c, :],
                                 start=(c == 0), stop=(c == C - 1))
                    ins.then_inc(s_y, 1)

            pe.wait_ge(s_cT, 16)
            context_qk()
            similarities(0, range(TC))
            pe.wait_ge(s_W, 64)
            for c in range(C):
                project(0, c)
            pe.wait_ge(s_sev, 6)
            context_qk()
            with pe.Fori(0, B - 1) as b:
                project(b + 1, 0)
                similarities(6 * b + 6, (0, 1))
                project(b + 1, 1)
                similarities(6 * b + 6, (2, 3))
                project(b + 1, 2)
                project(b + 1, 3)
                project_out(b)
                pe.wait_ge(s_cT, 16 * b + 32)
                pe.wait_ge(s_z, 4 * b + 4)
                context_qk()
            similarities(6 * B, range(TC))
            project_out(B - 1)


def block_c(nc, dram, x1_d, sim_d, m8, out):
    with ExitStack() as ctx:
        def sb(name, shape, dt=F32):
            return ctx.enter_context(nc.sbuf_tensor(name, shape, dt))

        def sem(name):
            return ctx.enter_context(nc.semaphore(name))

        vec = sb("vec", [P, NCOL])
        ident = sb("ident", [P, P])
        rope = sb("rope", [P, 4, T])
        causal = sb("causal", [P, P], F32R)
        identr = sb("identr", [P, P], F32R)
        before = sb("before", [P, TC, E, E])
        bo = sb("bo", [P, D])
        wg = sb("wg", [P, C, E])
        be2 = sb("be2", [E, D])
        gam = sb("gam", [P, 4])
        mhalf = sb("mhalf", [P, TC])
        ws = sb("ws", [P, 2, C * D])
        wh = sb("wh", [P, 4, C, D], F32R)
        wl = sb("wl", [P, 4, C, D], F32R)
        wgh = sb("wgh", [P, C, E], F32R)
        wgl = sb("wgl", [P, C, E], F32R)
        tk = sb("tk", [P, TC, T])
        thr = sb("thr", [P, TC])
        x2 = sb("x2", [P, TC, D])
        xn = sb("xn", [P, TC, D])
        xf = sb("xf", [P, 2, T])
        xh = sb("xh", [P, C, T], F32R)
        xl = sb("xl", [P, C, T], F32R)
        h = sb("h", [P, TC, D])
        st = sb("st", [P, TC, 6])
        mv = sb("mv", [P, TC, 2])
        var = sb("var", [P, TC])
        rstd = sb("rstd", [P, TC])
        sh = sb("sh", [P, 2, T])
        rc = sb("rc", [P, 2, T])
        qk = sb("qk", [P, 2, 2, T])
        Vg = sb("Vg", [P, TC, GH * P])
        Pr = sb("Pr", [P, TC, T])
        sx = Pr
        x1 = Vg
        nmax = sb("nmax", [P, TC])
        rsum = sb("rsum", [P, TC])
        rinv = sb("rinv", [P, TC])
        PT = sb("PT", [P, TC, T])
        tx = PT
        of = sb("of", [P, 2, T])
        oh = sb("oh", [P, GH, T], F32R)
        ol = sb("ol", [P, GH, T], F32R)
        lg = sb("lg", [P, 6, TC, E])
        r1 = sb("r1", [P, 6, TC])
        cmp_ = rc[:, 1, 0:3 * TC * E * E].rearrange("p (a t e j) -> p a t e j", a=3, t=TC, e=E)
        combT = rc[0:E, 0, :]
        ps = ctx.enter_context(nc.psum_tensor("ps", [P, 8, 512], F32))
        PJ, SA, SB, SC, PV = 0, 4, 5, 6, 7

        s_const = sem("c_const")
        s_pre = sem("c_pre")
        s_tanh = sem("c_tanh")
        s_half = sem("c_half")
        s_tkin = sem("c_tkin")
        s_tkdone = sem("c_tkdone")
        s_xin = sem("c_xin")
        s_xth = sem("c_xth")
        s_xA = sem("c_xA")
        s_xAT = sem("c_xAT")
        s_xATe = sem("c_xATe")
        s_var = sem("c_var")
        s_rstd = sem("c_rstd")
        s_xn = sem("c_xn")
        s_nT = sem("c_nT")
        s_nTe = sem("c_nTe")
        s_ws = [sem(f"c_ws{i}") for i in range(2)]
        s_wh = sem("c_wh")
        s_split = sem("c_split")
        s_xs = sem("c_xs")
        s_Oh = sem("c_Oh")
        s_Os = sem("c_Os")
        s_hs = sem("c_hs")
        s_QK = sem("c_QK")
        s_V = sem("c_V")
        s_Ve = sem("c_Ve")
        s_sh = sem("c_sh")
        s_rs = sem("c_rs")
        s_rope = sem("c_rope")
        s_S = sem("c_S")
        s_nm = sem("c_nm")
        s_P = sem("c_P")
        s_Pn = sem("c_Pn")
        s_T = sem("c_T")
        s_PT = sem("c_PT")
        s_PV = sem("c_PV")
        s_OT = sem("c_OT")
        s_O = sem("c_O")
        s_Oe = sem("c_Oe")
        s_lgT = sem("c_lgT")
        s_lgTe = sem("c_lgTe")
        s_lg = sem("c_lg")
        s_lge = sem("c_lge")
        s_lgx = sem("c_lgx")
        s_comb = sem("c_comb")
        s_cT = sem("c_cT")
        s_cTe = sem("c_cTe")
        s_h1 = sem("c_h1")
        s_gel = sem("c_gel")
        s_y = sem("c_y")
        s_ye = sem("c_ye")
        s_fin = sem("c_fin")
        s_out = sem("c_out")

        block = ctx.enter_context(nc.Block())

        @block.sync
        def _(sp):
            sp.dma_start(sx[:, :, :], sim_d[0]).then_inc(s_xin, 16)
            sp.dma_start(x1[:, :, :], x1_d[0]).then_inc(s_xin, 16)
            for dst, name in [(vec[:, :], "vec"), (ident[:, :], "ident"), (rope[:, :, :], "rope"),
                              (xf[:, 0, 0:P], "causal"), (before[:, :, :, :], "before"), (bo[:, :], "bo"),
                              (wg[:, :, :], "wg"), (be2[:, :], "be2")]:
                sp.dma_start(dst, dram[name]).then_inc(s_const, 16)

            def load(b, st, i):
                sp.wait_ge(s_split, MATS * b + 4 * st + i + 1)
                sp.dma_start(ws[:, i % 2, :], dram["wset"][st, i]).then_inc(s_ws[i % 2], 16)

            sp.dma_start(tk[:, :, :], sim_d[1]).then_inc(s_tkin, 16)
            with sp.Fori(0, B) as b:
                with sp.Fori(0, NG) as g:
                    for i in range(4):
                        load(b, g, i)
                for i in range(4):
                    load(b, NG, i)
                sp.wait_ge(s_PV, 16 * b + 16)
                sp.dma_start(sx[:, :, :], sim_d[(b + 1) % B]).then_inc(s_xin, 16)
                sp.dma_start(x1[:, :, :], x1_d[(b + 1) % B]).then_inc(s_xin, 16)
                sp.wait_ge(s_tkdone, b + 2)
                sp.dma_start(tk[:, :, :], sim_d[(b + 2) % B]).then_inc(s_tkin, 16)
                for i in range(4):
                    load(b, NG + 1, i)
            for i in range(4):
                load(B, 0, i)
            sp.wait_ge(s_tkin, 16 * B + 16)

        @block.gpsimd
        def _(pool):
            nc.gpsimd.memset(mhalf[:, :], -0.5).then_inc(s_half, 1)
            pool.wait_ge(s_half, 1)
            pool.wait_ge(s_const, 128)
            pool.sem_inc(s_split, 2)
            pool.sem_inc(s_Os, 2)

            def root(n):
                pool.wait_ge(s_var, n)
                nc.gpsimd.tensor_tensor(rstd[:, :], var[:, :], mhalf[:, :], ALU.pow).then_inc(s_rstd, 1)

            def sines(n, a):
                pool.wait_ge(s_sh, 2 * n + a + 1)
                nc.gpsimd.tensor_tensor(sh[:, a, :], sh[:, a, :], rope[:, 2 * a + 1, :], ALU.mult).then_inc(s_rs, 1)


            def weight_lo(K, i):
                pool.wait_ge(s_wh, K + 1)
                nc.gpsimd.tensor_tensor(wl[:, SLOTS[i], :, :].rearrange("p c n -> p (c n)"), ws[:, i % 2, :],
                                        wh[:, SLOTS[i], :, :].rearrange("p c n -> p (c n)"),
                                        ALU.subtract).then_inc(s_split, 1)

            def head_lo(n, hh):
                pool.wait_ge(s_Oh, n + 1)
                nc.gpsimd.tensor_tensor(ol[:, hh, :], of[:, hh % 2, :], oh[:, hh, :], ALU.subtract).then_inc(s_Os, 1)

            root(1)
            weight_lo(0, 0)
            root(2)
            weight_lo(1, 1)
            weight_lo(2, 2)
            with pool.Fori(0, B) as b:
                with pool.Fori(0, NG) as g:
                    G = b * NG + g
                    K = MATS * b + 4 * g + 4

                    def both_sines(hh):
                        sines(4 * G + hh, 0)
                        sines(4 * G + hh, 1)
                    both_sines(0)
                    both_sines(1)
                    weight_lo(K - 1, 3)
                    head_lo(4 * G, 0)
                    weight_lo(K, 0)
                    both_sines(2)
                    head_lo(4 * G + 1, 1)
                    both_sines(3)
                    head_lo(4 * G + 2, 2)
                    weight_lo(K + 1, 1)
                    weight_lo(K + 2, 2)
                    head_lo(4 * G + 3, 3)
                K = MATS * b + 4 * NG + 4
                root(4 * b + 3)
                weight_lo(K - 1, 3)
                weight_lo(K, 0)
                weight_lo(K + 1, 1)
                weight_lo(K + 2, 2)
                root(4 * b + 4)
                weight_lo(K + 3, 3)
                weight_lo(K + 4, 0)
                root(4 * b + 5)
                weight_lo(K + 5, 1)
                weight_lo(K + 6, 2)
                root(4 * b + 6)
            weight_lo(MATS * B + 3, 3)

        @block.scalar
        def _(act):
            A = nc.scalar.activation

            def half_tanh(k):
                act.wait_ge(s_xin, 32 * k + 32)
                for t in range(TC):
                    A(tx[:, t, :], sx[:, t, :], ACT.Tanh, scale=0.5).then_inc(s_xth, 1)

            half_tanh(0)
            act.wait_ge(s_const, 128)
            A(gam[:, 2:3], vec[:, COL["gamma"]:COL["gamma"] + 1], ACT.Tanh, scale=0.5).then_inc(s_tanh, 1)
            act.sem_inc(s_OT, 1)
            act.sem_inc(s_gel, 4)
            act.sem_inc(s_out, 16)

            def col(name, i):
                return vec[:, COL[name] + i:COL[name] + i + 1]

            def weight_hi(K, i):
                act.wait_ge(s_ws[i % 2], 16 * K_half(K, i) + 16)
                nc.scalar.copy(wh[:, SLOTS[i], :, :].rearrange("p c n -> p (c n)"), ws[:, i % 2, :]).then_inc(s_wh, 1)

            def K_half(K, i):
                return K + i // 2

            def swapped(G, hh, a):
                n = 4 * G + hh
                bank = PJ + 2 * (hh % 2) + a
                bias = vec[:, bass.ds(COL["bq"] + 16 * a + n_head(hh), 1)]
                act.wait_ge(s_QK, 8 * G + 8 + 2 * hh + a + 1)
                act.wait_ge(s_rope, 2 * n + 1 + a)
                A(sh[0:64, a, :], ps[64:128, bank, :], ACT.Identity, bias=bias[64:128, :])
                A(sh[64:128, a, :], ps[0:64, bank, :], ACT.Identity, bias=bias[0:64, :]).then_inc(s_sh, 1)

            def exps(n):
                for t in range(TC):
                    act.wait_ge(s_nm, 4 * n + max(t, 1) + 1)
                    A(Pr[:, t, 0:(t + 1) * P], s_tile(t), ACT.Exp, bias=nmax[:, t:t + 1],
                      accum_out=rsum[:, t:t + 1]).then_inc(s_P, 1)

            def s_tile(t):
                return [ps[:, SA, 0:P], ps[:, SA, P:3 * P], ps[:, SB, 0:3 * P], ps[:, SC, 0:4 * P]][t]

            def pt_out(n):
                act.wait_ge(s_T, 3 * n + 1)
                nc.scalar.copy(PT[:, 0, :], ps[:, SA, :]).then_inc(s_PT, 1)
                act.wait_ge(s_T, 3 * n + 2)
                nc.scalar.copy(PT[:, 1, P:T], ps[:, SB, 0:3 * P])
                nc.scalar.copy(PT[:, 3, 3 * P:T], ps[:, SB, 3 * P:T]).then_inc(s_PT, 1)
                act.wait_ge(s_T, 3 * n + 3)
                nc.scalar.copy(PT[:, 2, 2 * P:T], ps[:, SC, 0:2 * P]).then_inc(s_PT, 1)

            def ot_out(n, g, hh):
                act.wait_ge(s_Os, n + 1)
                act.wait_ge(s_PV, n + 1)
                A(of[:, hh % 2, :], ps[:, PV, :], ACT.Identity,
                  bias=vec[:, bass.ds(COL["bv"] + 4 * g + hh, 1)]).then_inc(s_OT, 1)
                act.drain()
                nc.scalar.copy(oh[:, hh, :], of[:, hh % 2, :]).then_inc(s_Oh, 1)

            def normed(b, which, lnw, lnb):
                for c in range(C):
                    if c >= 2:
                        act.wait_ge(s_xs, 8 * b + 4 * which + c - 1)
                    act.wait_ge(s_nT, 8 * b + 4 * which + c + 1)
                    A(xf[:, c % 2, :], ps[:, PJ + c, :], ACT.Identity, bias=col(lnb, c),
                      scale=col(lnw, c)).then_inc(s_nTe, 1)

            for i in range(3):
                weight_hi(0, i)
            normed(0, 0, "ln1w", "ln1b")
            weight_hi(0, 3)
            with act.Fori(0, B) as b:
                with act.Fori(0, NG) as g:
                    G = b * NG + g

                    def n_head(hh):
                        return 4 * g + hh
                    K2 = MATS // 2 * b + 2 * g + 2
                    for hh in range(2):
                        swapped(G, hh, 0)
                        swapped(G, hh, 1)
                    for hh in range(GH):
                        n = 4 * G + hh
                        exps(n)
                        if hh == 0:
                            for t in range(TC):
                                act.wait_ge(s_V, 4 * G + 4 + t + 1)
                                nc.scalar.copy(Vg[:, t, :], ps[:, PJ + t, :]).then_inc(s_Ve, 1)
                            weight_hi(K2, 0)
                        if 1 <= hh < 3:
                            swapped(G, hh + 1, 0)
                            swapped(G, hh + 1, 1)
                        if hh == 0:
                            act.wait_ge(s_out, 16 * b + 16)
                        pt_out(n)
                        ot_out(n, g, hh)
                        if hh == 2:
                            weight_hi(K2, 1)
                            weight_hi(K2, 2)
                    act.wait_ge(s_O, 4 * G + 8)
                    weight_hi(K2, 3)
                normed(b, 1, "ln2w", "ln2b")
                act.wait_ge(s_lgT, b + 1)
                nc.scalar.copy(combT[:, :], ps[0:E, SA, :]).then_inc(s_lgTe, 1)
                for i in range(2):
                    act.wait_ge(s_lge, 2 * b + i + 1)
                    A(lg[:, 2 + 2 * i, :, :], lg[:, 1 + 2 * i, :, :], ACT.Exp).then_inc(s_lgx, 1)
                half_tanh(b + 1)
                act.wait_ge(s_cT, b + 1)
                nc.scalar.copy(combT[:, :], ps[0:E, SB, :]).then_inc(s_cTe, 1)
                K2 = MATS // 2 * b + 2 * NG + 2
                for e in range(E):
                    for i in range(C):
                        act.wait_ge(s_hs, 16 * b + 4 * e + i + 3)
                        act.wait_ge(s_h1, 16 * b + 4 * e + i + 5)
                        A(of[:, i % 2, :], ps[:, PJ + i, :], ACT.Gelu,
                          bias=col("be1", 4 * e + i)).then_inc(s_gel, 1)
                    weight_hi(K2 + 2 * (e // 2), 2 * (e % 2))
                    if e == E - 1:
                        normed(b + 1, 0, "ln1w", "ln1b")
                    act.wait_ge(s_y, 20 * b + 4 * e + 12)
                    weight_hi(K2 + 2 * (e // 2), 2 * (e % 2) + 1)
                act.wait_ge(s_fin, b + 1)
                act.dma_start(out[b], tx[:, :, :]).then_inc(s_out, 16)
            act.wait_ge(s_out, 16 * B + 16)

        @block.vector
        def _(dve):
            v = nc.vector

            def split_normed(k, which):
                for c in range(C):
                    dve.wait_ge(s_nTe, 8 * k + 4 * which + c + 1)
                    v.tensor_copy(xh[:, c, :], xf[:, c % 2, :])
                    v.drain()
                    v.tensor_tensor(xl[:, c, :], xf[:, c % 2, :], xh[:, c, :], ALU.subtract).then_inc(s_xs, 1)

            def split_hidden(b, e):
                for i in range(C):
                    dve.wait_ge(s_gel, 16 * b + 4 * e + i + 5)
                    v.tensor_copy(oh[:, i, :], of[:, i % 2, :])
                    v.drain()
                    v.tensor_tensor(ol[:, i, :], of[:, i % 2, :], oh[:, i, :], ALU.subtract).then_inc(s_hs, 1)

            def layer_norm(k, src, dst, done=None):
                v.drain()
                for t in range(TC):
                    v.bn_stats(st[:, t, :], src[:, t, :])
                v.drain()
                for t in range(TC):
                    v.bn_aggr(mv[:, t, :], st[:, t, :])
                v.drain()
                v.tensor_scalar(var[:, :], mv[:, :, 1], EPS, None, ALU.add).then_inc(s_var, 1)
                dve.wait_ge(s_rstd, k)
                for t in range(TC):
                    ins = v.tensor_scalar(dst[:, t, :], src[:, t, :], mv[:, t, 0:1], rstd[:, t:t + 1],
                                          ALU.subtract, ALU.mult)
                    if done is not None:
                        ins.then_inc(done, 1)
                return ins

            def s_tile(t):
                return [ps[:, SA, 0:P], ps[:, SA, P:3 * P], ps[:, SB, 0:3 * P], ps[:, SC, 0:4 * P]][t]

            def rotate(G, g, hh, a):
                n = 4 * G + hh
                bank = PJ + 2 * (hh % 2) + a
                dve.wait_ge(s_sh, 2 * n + a + 1)
                v.scalar_tensor_tensor(rc[:, a, :], ps[:, bank, :], vec[:, bass.ds(COL["bq"] + 16 * a + 4 * g + hh, 1)],
                                       rope[:, 2 * a, :], ALU.add, ALU.mult)
                v.drain()
                dve.wait_ge(s_rs, 2 * n + a + 1)
                v.tensor_tensor(qk[:, hh % 2, a, :], rc[:, a, :], sh[:, a, :], ALU.add).then_inc(s_rope, 1)

            def maxima(n):
                for t in range(TC):
                    if t != 1:
                        dve.wait_ge(s_S, 4 * n + max(t, 1) + 1)
                    v.tensor_reduce(nmax[:, t:t + 1], s_tile(t), AX.X, ALU.max, negate=True).then_inc(s_nm, 1)

            def normalise(n):
                for t0 in (0, 2):
                    dve.wait_ge(s_P, 4 * n + t0 + 2)
                    v.reciprocal(rinv[:, t0:t0 + 2], rsum[:, t0:t0 + 2])
                    v.drain()
                    for t in (t0, t0 + 1):
                        ins = v.tensor_scalar(Pr[:, t, 0:(t + 1) * P], Pr[:, t, 0:(t + 1) * P], rinv[:, t:t + 1],
                                              None, ALU.mult)
                ins.then_inc(s_Pn, 1)

            def search(first, count):
                for i in range(first, first + count):
                    take_largest(nc, m8, tk, [i // RPG], 1)

            def threshold(k):
                v.drain()
                v.tensor_copy(thr[:, :], m8[:, :, KTH]).then_inc(s_tkdone, 1)

            def adjacency(k):
                for t in range(TC):
                    dve.wait_ge(s_xth, 4 * k + t + 1)
                    v.tensor_scalar(tx[:, t, :], tx[:, t, :], 1.0, None, ALU.add)
                v.drain()
                for t in range(TC):
                    v.scalar_tensor_tensor(sx[:, t, :], sx[:, t, :], thr[:, t:t + 1], tx[:, t, :], ALU.is_ge,
                                           ALU.mult).then_inc(s_xA, 1)
                v.drain()

            def symmetric(k):
                for t in range(TC):
                    dve.wait_ge(s_xAT, 4 * k + t + 1)
                    v.tensor_tensor(tx[:, t, :], ps[:, PJ + t, :], sx[:, t, :], ALU.add).then_inc(s_xATe, 1)
                v.drain()
                for t in range(TC):
                    v.tensor_scalar(tx[:, t, :], tx[:, t, :], gam[:, 0:1], None, ALU.mult)
                v.drain()
                for t in range(TC):
                    v.scalar_tensor_tensor(x2[:, t, :], x1[:, t, :], gam[:, 1:2], tx[:, t, :], ALU.mult, ALU.add)

            threshold(0)
            adjacency(0)
            dve.wait_ge(s_const, 128)
            dve.wait_ge(s_tanh, 1)
            v.tensor_scalar(gam[:, 0:1], gam[:, 2:3], 1.0, 0.125, ALU.add, ALU.mult)
            v.tensor_scalar(gam[:, 1:2], gam[:, 2:3], -0.5, 1.5, ALU.mult, ALU.add)
            dve.sem_inc(s_rope, 2)
            dve.sem_inc(s_Oe, 4)
            dve.sem_inc(s_ye, 4)
            dve.sem_inc(s_hs, 4)

            v.tensor_copy(causal[:, :], xf[:, 0, 0:P])
            v.tensor_copy(identr[:, :], ident[:, :]).then_inc(s_pre, 1)
            v.tensor_copy(wgh[:, :, :], wg[:, :, :])
            v.drain()
            v.tensor_tensor(wgl[:, :, :], wg[:, :, :], wgh[:, :, :], ALU.subtract)
            symmetric(0)
            layer_norm(1, x2, x2)
            layer_norm(2, x2, xn, s_xn)
            split_normed(0, 0)
            dve.wait_ge(s_tkin, 16)
            for t in range(TC):
                v.tensor_tensor(h[:, t, :], x2[:, t, :], bo[:, :], ALU.add)
            with dve.Fori(0, B) as b:
                with dve.Fori(0, NG) as g:
                    G = b * NG + g
                    search(0, START)
                    for hh in range(2):
                        rotate(G, g, hh, 0)
                        rotate(G, g, hh, 1)
                    for hh in range(GH):
                        n = 4 * G + hh
                        maxima(n)
                        search(START + sum(BEFORE[:hh]) + sum(AFTER[:hh]), BEFORE[hh])
                        normalise(n)
                        if 1 <= hh < 3:
                            rotate(G, g, hh + 1, 0)
                            rotate(G, g, hh + 1, 1)
                        search(START + sum(BEFORE[:hh + 1]) + sum(AFTER[:hh]), AFTER[hh])
                    for t in range(TC):
                        dve.wait_ge(s_O, 4 * G + t + 5)
                        v.tensor_tensor(h[:, t, :], ps[:, PJ + t, :], h[:, t, :], ALU.add).then_inc(s_Oe, 1)
                layer_norm(4 * b + 3, h, xn, s_xn)
                split_normed(b, 1)
                for t in range(TC):
                    v.tensor_tensor(h[:, t, :], x2[:, t, :], h[:, t, :], ALU.add)
                threshold(b + 1)

                def over(x):
                    return x.rearrange("p (t o) -> p t o", o=1).to_broadcast([P, TC, E])
                dve.wait_ge(s_lg, b + 1)
                v.tensor_copy(lg[:, 0, :, :], ps[:, SC, 0:TC * E].rearrange("p (t e) -> p t e", e=E))
                v.drain()
                v.tensor_reduce(r1[:, 0, :], lg[:, 0, :, :], AX.X, ALU.max)
                v.drain()
                v.tensor_tensor(lg[:, 1, :, :], lg[:, 0, :, :], over(r1[:, 0, :]), ALU.subtract).then_inc(s_lge, 1)
                dve.wait_ge(s_lgx, 2 * b + 1)
                v.tensor_reduce(r1[:, 1, :], lg[:, 2, :, :], AX.X, ALU.add)
                v.drain()
                v.reciprocal(r1[:, 2, :], r1[:, 1, :])
                v.drain()
                v.tensor_tensor(lg[:, 0, :, :], lg[:, 2, :, :], over(r1[:, 2, :]), ALU.mult)
                v.drain()
                v.tensor_reduce(r1[:, 3, :], lg[:, 0, :, :], AX.X, ALU.max)
                for j in range(E):
                    pj = lg[:, 0, :, j:j + 1].to_broadcast([P, TC, E])
                    v.tensor_tensor(cmp_[:, 0, :, :, j], pj, lg[:, 0, :, :], ALU.is_gt)
                    v.tensor_tensor(cmp_[:, 1, :, :, j], pj, lg[:, 0, :, :], ALU.is_equal)
                v.drain()
                v.tensor_tensor(cmp_[:, 2, :, :, :], cmp_[:, 1, :, :, :], before[:, :, :, :], ALU.mult)
                v.tensor_tensor(lg[:, 3, :, :], lg[:, 0, :, :], over(r1[:, 3, :]), ALU.subtract).then_inc(s_lge, 1)
                v.drain()
                v.tensor_tensor(cmp_[:, 1, :, :, :], cmp_[:, 0, :, :, :], cmp_[:, 2, :, :, :], ALU.add)
                v.drain()
                v.tensor_reduce(lg[:, 5, :, :], cmp_[:, 1, :, :, :], AX.X, ALU.add)
                v.drain()
                dve.wait_ge(s_lgx, 2 * b + 2)
                v.scalar_tensor_tensor(lg[:, 1, :, :], lg[:, 5, :, :], 2.0, lg[:, 4, :, :], ALU.is_lt, ALU.mult)
                v.drain()
                v.tensor_reduce(r1[:, 4, :], lg[:, 1, :, :], AX.X, ALU.add)
                v.drain()
                v.reciprocal(r1[:, 5, :], r1[:, 4, :])
                v.drain()
                v.tensor_tensor(lg[:, 5, :, :], lg[:, 1, :, :], over(r1[:, 5, :]), ALU.mult).then_inc(s_comb, 1)

                def add_expert(e):
                    for t in range(TC):
                        v.drain()
                        dve.wait_ge(s_y, 20 * b + 4 * e + t + 9)
                        v.scalar_tensor_tensor(h[:, t, :], ps[:, SA + t, :], lg[:, 5, t, e:e + 1], h[:, t, :],
                                               ALU.mult, ALU.add).then_inc(s_ye, 1)

                adjacency(b + 1)
                for t in range(TC):
                    dve.wait_ge(s_y, 20 * b + t + 5)
                    v.tensor_tensor(h[:, t, :], ps[:, SA + t, :], h[:, t, :], ALU.add).then_inc(s_ye, 1)
                split_hidden(b, 0)
                symmetric(b + 1)
                add_expert(0)
                split_hidden(b, 1)
                layer_norm(4 * b + 4, x2, x2)
                add_expert(1)
                split_hidden(b, 2)
                layer_norm(4 * b + 5, x2, xn, s_xn)
                add_expert(2)
                split_hidden(b, 3)
                split_normed(b + 1, 0)
                add_expert(3)
                layer_norm(4 * b + 6, h, tx).then_inc(s_fin, 1)
                v.drain()
                dve.wait_ge(s_tkin, 16 * b + 32)
                for t in range(TC):
                    v.tensor_tensor(h[:, t, :], x2[:, t, :], bo[:, :], ALU.add)

        @block.tensor
        def _(pe):
            mm = nc.tensor.matmul
            tr = nc.tensor.transpose
            pe.wait_ge(s_const, 128)
            pe.wait_ge(s_pre, 1)
            pe.sem_inc(s_QK, 8)
            pe.sem_inc(s_V, 4)
            pe.sem_inc(s_O, 4)
            pe.sem_inc(s_h1, 4)
            pe.sem_inc(s_y, 4)

            def product(dst, terms, first=True, last=True):
                for j, (ah, al, bh, bl) in enumerate(terms):
                    start, stop = first and j == 0, last and j == len(terms) - 1
                    mm(dst, ah, bh, start=start, stop=False, skip_group_check=True)
                    mm(dst, ah, bl, start=False, stop=False, skip_group_check=True)
                    ins = mm(dst, al, bh, start=False, stop=stop, skip_group_check=True)
                return ins

            def ready(K):
                pe.wait_ge(s_split, K + 3)

            def transposed(b, which):
                for t in range(TC):
                    pe.wait_ge(s_xn, 8 * b + 4 * which + t + 1)
                    for c in range(C):
                        ins = tr(ps[:, PJ + c, t * P:(t + 1) * P], xn[:, t, c * P:(c + 1) * P], ident[:, :])
                        if t == TC - 1:
                            ins.then_inc(s_nT, 1)

            def project_qk(G, K, hh):
                for a in range(2):
                    bank = PJ + 2 * (hh % 2) + a
                    if hh < 2:
                        pe.wait_ge(s_Oe, 4 * G + 2 * hh + a + 1)
                    else:
                        pe.wait_ge(s_Ve, 4 * G + 2 * (hh - 2) + a + 1)
                    if hh == 0:
                        ready(K + 1 + a)
                    cols = slice(hh * P, (hh + 1) * P)
                    for k in range(C):
                        if hh == a == 0:
                            pe.wait_ge(s_xs, 8 * b + k + 1)
                        ins = product(ps[:, bank, :], [(wh[:, a, k, cols], wl[:, a, k, cols], xh[:, k, :],
                                                        xl[:, k, :])], first=k == 0, last=k == C - 1)
                    ins.then_inc(s_QK, 1)

            def scores(n, hh):
                pe.wait_ge(s_rope, 2 * n + 4)
                q, k = qk[:, hh % 2, 0, :], qk[:, hh % 2, 1, :]
                for t, dst in enumerate([ps[:, SA, 0:P], ps[:, SA, P:3 * P], ps[:, SB, 0:3 * P], ps[:, SC, 0:4 * P]]):
                    mm(dst, q[:, t * P:(t + 1) * P], k[:, 0:(t + 1) * P], start=True, stop=False,
                       skip_group_check=True)
                    mm(dst[:, t * P:(t + 1) * P], identr[:, :], causal[:, :], start=False, stop=True,
                       skip_group_check=True).then_inc(s_S, 1)

            def values(G):
                for t in range(TC):
                    pe.wait_ge(s_rope, 8 * G + t + 3)
                    rows = slice(t * P, (t + 1) * P)
                    product(ps[:, PJ + t, :], [(xh[:, k, rows], xl[:, k, rows], wh[:, 2, k, :], wl[:, 2, k, :])
                                               for k in range(C)]).then_inc(s_V, 1)

            def transpose_probs(n):
                pe.wait_ge(s_Pn, n + 1)
                for t in range(TC):
                    ins = tr(ps[:, SA, t * P:(t + 1) * P], Pr[:, t, 0:P], ident[:, :])
                ins.then_inc(s_T, 1)
                for t in range(1, TC):
                    tr(ps[:, SB, (t - 1) * P:t * P], Pr[:, t, P:2 * P], ident[:, :])
                tr(ps[:, SB, 3 * P:T], Pr[:, 3, 3 * P:T], ident[:, :]).then_inc(s_T, 1)
                for t in range(2, TC):
                    ins = tr(ps[:, SC, (t - 2) * P:(t - 1) * P], Pr[:, t, 2 * P:3 * P], ident[:, :])
                ins.then_inc(s_T, 1)

            def weigh_values(G, n, hh):
                if hh == 0:
                    pe.wait_ge(s_Ve, 4 * G + 4)
                pe.wait_ge(s_OT, n + 1)
                for i, j in enumerate((0, 1, 3, 2)):
                    pe.wait_ge(s_PT, 3 * n + (1, 2, 2, 3)[i])
                    ins = mm(ps[:, PV, j * P:T], Vg[:, j, hh * P:(hh + 1) * P], PT[:, j, j * P:T], start=(i == 0),
                             stop=(i == 3), skip_group_check=True)
                ins.then_inc(s_PV, 1)

            def project_out(G):
                for t in range(TC):
                    pe.wait_ge(s_rope, 8 * G + t + 7)
                    rows = slice(t * P, (t + 1) * P)
                    product(ps[:, PJ + t, :], [(oh[:, hh, rows], ol[:, hh, rows], wh[:, 3, hh, :],
                                                wl[:, 3, hh, :]) for hh in range(GH - 1)], last=False)

            def transposed_adjacency(k):
                pe.wait_ge(s_xA, 4 * k + 4)
                for t in range(TC):
                    for m in range(TC):
                        ins = tr(ps[:, PJ + t, m * P:(m + 1) * P], sx[:, m, t * P:(t + 1) * P], ident[:, :])
                    ins.then_inc(s_xAT, 1)

            transposed_adjacency(0)
            transposed(0, 0)
            with pe.Fori(0, B) as b:
                with pe.Fori(0, NG) as g:
                    G = b * NG + g
                    K = MATS * b + 4 * g
                    project_qk(G, K, 0)
                    project_qk(G, K, 1)
                    for hh in range(GH):
                        n = 4 * G + hh
                        scores(n, hh)
                        if hh == 0:
                            values(G)
                        elif hh < 3:
                            project_qk(G, K, hh + 1)
                        else:
                            ready(K + 3)
                            pe.wait_ge(s_Os, n + 2)
                            project_out(G)
                        transpose_probs(n)
                        weigh_values(G, n, hh)
                    pe.wait_ge(s_Oh, 4 * G + 4)
                    for t in range(TC):
                        rows = slice(t * P, (t + 1) * P)
                        for w in (wh, wl):
                            mm(ps[:, PJ + t, :], oh[:, 3, rows], w[:, 3, 3, :], start=False, stop=False,
                               skip_group_check=True)
                    pe.wait_ge(s_Os, 4 * G + 6)
                    for t in range(TC):
                        mm(ps[:, PJ + t, :], ol[:, 3, t * P:(t + 1) * P], wh[:, 3, 3, :], start=False, stop=True,
                           skip_group_check=True).then_inc(s_O, 1)
                transposed(b, 1)
                for k in range(C):
                    pe.wait_ge(s_xs, 8 * b + k + 5)
                    ins = product(ps[0:E, SA, :], [(wgh[:, k, :], wgl[:, k, :], xh[:, k, :], xl[:, k, :])],
                                  first=k == 0, last=k == C - 1)
                ins.then_inc(s_lgT, 1)

                KE = MATS * b + 4 * NG

                def expert_in(e, chunks=range(C)):
                    ready(KE + 2 * e)
                    slot = (2, 1)[e % 2]
                    for i in chunks:
                        pe.wait_ge(s_gel, 16 * b + 4 * e + i + 1)
                        if e == 1:
                            pe.wait_ge(s_xATe, 4 * b + i + 5)
                        cols = slice(i * P, (i + 1) * P)
                        product(ps[:, PJ + i, :], [(wh[:, slot, k, cols], wl[:, slot, k, cols], xh[:, k, :],
                                                    xl[:, k, :]) for k in range(C)]).then_inc(s_h1, 1)

                def expert_out(e):
                    ready(KE + 2 * e + 1)
                    slot = (0, 3)[e % 2]
                    pe.wait_ge(s_hs, 16 * b + 4 * e + 8)
                    for t in range(TC):
                        pe.wait_ge(s_ye, 20 * b + 4 * e + t + 5)
                        rows = slice(t * P, (t + 1) * P)
                        product(ps[:, SA + t, :], [(oh[:, i, rows], ol[:, i, rows], wh[:, slot, i, :],
                                                    wl[:, slot, i, :]) for i in range(C)]).then_inc(s_y, 1)

                pe.wait_ge(s_lgTe, b + 1)
                expert_in(0, [0])
                for t in range(TC):
                    ins = tr(ps[:, SC, t * E:(t + 1) * E], combT[:, t * P:(t + 1) * P], ident[0:E, 0:E])
                ins.then_inc(s_lg, 1)
                expert_in(0, range(1, C))
                pe.wait_ge(s_comb, b + 1)
                for t in range(TC):
                    ins = tr(ps[0:E, SB, t * P:(t + 1) * P], lg[:, 5, t, :], ident[:, :])
                ins.then_inc(s_cT, 1)
                pe.wait_ge(s_cTe, b + 1)
                for t in range(TC):
                    mm(ps[:, SA + t, :], combT[:, t * P:(t + 1) * P], be2[:, :], start=True, stop=True).then_inc(s_y, 1)
                pe.wait_ge(s_gel, 16 * b + 8)
                transposed_adjacency(b + 1)
                expert_out(0)
                for e in range(1, E):
                    expert_in(e)
                    if e == E - 1:
                        pe.wait_ge(s_gel, 16 * b + 20)
                        transposed(b + 1, 0)
                    expert_out(e)


def decoder(nc, dram, out):
    x1_d = nc.dram_tensor("x1_scratch", (B, P, TC, D), F32, kind="Internal").ap()
    sim_d = nc.dram_tensor("sim_scratch", (B, P, TC, T), F32, kind="Internal").ap()
    with nc.sbuf_tensor("m8", [P, TC, 8], F32) as m8:
        block_a(nc, dram, x1_d, sim_d, m8)
        block_c(nc, dram, x1_d, sim_d, m8, out)


def rope_tables():
    f = np.float32
    inv = f(1.0) / np.power(f(10000.0), np.arange(0, P, 2, dtype=f) / f(P)).astype(f)
    ang = (np.arange(T, dtype=f)[:, None] * inv[None, :]).astype(f)
    ang = np.concatenate([ang, ang], 1).T
    cos, sin = np.cos(ang).astype(f), np.sin(ang).astype(f)
    sin[:P // 2] *= -1
    s = f(P ** -0.5)
    return np.ascontiguousarray(np.stack([cos * s, sin * s, cos, sin], 1))


def kernel(**inputs):
    from concourse import bacc
    from concourse.bass_utils import run_bass_kernel_spmd

    a = {k: np.asarray(v) for k, v in inputs.items()}

    def rows(w):
        return w.reshape(-1, P, w.shape[-1]).transpose(1, 0, 2)

    def feat(w):
        return w.reshape(-1, P).T

    def tokens(x):
        return x.reshape(B, TC, P, -1).transpose(0, 2, 1, 3)

    f = "L0_ffn_"
    r = "L0_attn_"
    vec = np.concatenate(
        [feat(a[r + "time_mix_" + n]) for n in ("key", "value", "receptance")]
        + [feat(a[r + "time_decay"]), feat(a[r + "time_first"])]
        + [feat(a[f + n]) for n in ("bq", "bk", "bv", "ln1_w", "ln1_b", "ln2_w", "ln2_b", "be1")]
        + [np.broadcast_to(a["L0_xattn_gamma_raw"].reshape(1, 1), (P, 1))], axis=1)
    xT = a["x"].reshape(B, T, C, P).transpose(0, 3, 2, 1)
    groups = (C, P, NG, GH * P)
    by_group = np.stack([a[f + n].reshape(groups).transpose(2, 1, 0, 3) for n in ("wv", "wq", "wk")]
                        + [a[f + "wo"].reshape(NG, GH, P, D).transpose(0, 2, 1, 3)], 1)
    by_expert = np.stack([w.reshape(E, C, P, D).transpose(0, 2, 1, 3) for w in (a[f + "we1"], a[f + "we2"])], 1)
    by_expert = by_expert.reshape(E // 2, 4, P, C, D)
    before = np.broadcast_to((np.arange(E)[None, :] < np.arange(E)[:, None]).astype(np.float32), (P, TC, E, E))
    q = np.arange(P)
    arrays = {
        "vec": vec,
        "wqkT": np.stack([a["L0_xattn_Wq"].T, a["L0_xattn_Wk"].T], 1),
        "W": np.stack([rows(a[r + n]) for n in ("Wk", "Wv", "Wr", "Wo")]),
        "x": tokens(a["x"]),
        "xT": np.pad(xT, ((0, 0), (0, 0), (0, 0), (1, 0))),
        "cT": a["ctx_512"].transpose(0, 2, 1),
        "ident": np.eye(P, dtype=np.float32),
        "rope": rope_tables(),
        "causal": np.where(q[None, :] > q[:, None], np.float32(NEG), np.float32(0)),
        "before": before,
        "bo": np.broadcast_to(a[f + "bo"], (P, D)),
        "wg": rows(a[f + "w_gate"]),
        "be2": a[f + "be2"],
        "wset": np.concatenate([by_group, by_expert]).reshape(SETS, 4, P, C * D),
    }
    arrays = {k: np.ascontiguousarray(w) for k, w in arrays.items()}
    nc = bacc.Bacc("TRN2", target_bir_lowering=False, num_devices=1)
    dram = {k: nc.dram_tensor("in_" + k, w.shape, mybir.dt.from_np(w.dtype), kind="ExternalInput").ap()
            for k, w in arrays.items()}
    out = nc.dram_tensor("out_x", (B, P, TC, D), F32, kind="ExternalOutput").ap()
    decoder(nc, dram, out)
    res = run_bass_kernel_spmd(nc, [{"in_" + k: w for k, w in arrays.items()}], core_ids=[0])
    y = res.results[0]["out_x"]
    return y.transpose(0, 2, 1, 3).reshape(B, T, D)
```
